# Optimizing a Trainium2 kernel written in Bass

```python
import numpy as np
import jax
import jax.numpy as jnp

def _softmax(x, axis=-1):
    return jax.nn.softmax(x, axis=axis)

def _gelu(x):
    return jax.nn.gelu(x, approximate=True)

def _silu(x):
    return jax.nn.silu(x)

def _sigmoid(x):
    return jax.nn.sigmoid(x)

def _layernorm(x, axis=-1, eps=1e-05):
    m = jnp.mean(x, axis=axis, keepdims=True)
    v = jnp.var(x, axis=axis, keepdims=True)
    return (x - m) / jnp.sqrt(v + eps)

def _scatter_add(tgt, idx, src, axis=0):
    return tgt.at[idx].add(src)

def _segment_sum(src, seg, n):
    return jax.ops.segment_sum(src, seg, n)
kernel_name = 'mk_cond_resid_d2_seqx_r8_276435'

def setup_inputs(seed: int=0):
    np.random.seed(seed)
    _w = jnp.asarray

    def _rec_inputs():
        import jax
        import jax.numpy as jnp
        _rk = jax.random.key(seed)
        x = -7.109e-05 + 0.9999 * jax.random.normal(jax.random.fold_in(_rk, 1), (128, 32, 256), jnp.float32)
        _lenS = 32 - jax.random.randint(jax.random.fold_in(_rk, 7), (128,), 0, max(1, 32 // 4) + 1, jnp.int32)
        _lenS2 = 32 - jax.random.randint(jax.random.fold_in(_rk, 8), (128,), 0, max(1, 32 // 4) + 1, jnp.int32)
        itok_B_1_198 = jax.random.randint(jax.random.fold_in(_rk, 11), (128,), 1, 199, jnp.int32)
        itok_Bx257_0_4111 = jax.random.randint(jax.random.fold_in(_rk, 12), (128, 257), 0, 514, jnp.int32)
        itok_B_37_3939 = jax.random.randint(jax.random.fold_in(_rk, 13), (128,), 37, 3940, jnp.int32)
        return (x, itok_B_1_198, itok_Bx257_0_4111, itok_B_37_3939)
    x, itok_B_1_198, itok_Bx257_0_4111, itok_B_37_3939 = _rec_inputs()

    def _L0_cond_setup():
        import jax, jax.numpy as jnp
        import numpy as np
        B, C, T = (128, 32, 256)
        S, D = (200, 32)
        key = jax.random.key(seed)
        k1, k2, k3 = jax.random.split(key, 3)
        x = jax.random.normal(k1, (B, C, T), dtype=jnp.float32)
        conditions = jax.random.randint(k2, (B,), 0, S, dtype=jnp.int64)
        weights = jax.random.normal(k3, (S, C, D), dtype=jnp.float32) / jnp.sqrt(jnp.float32(C))
        return {'x': x, 'conditions': conditions, 'weights': weights}
    _L0_cond_all = _L0_cond_setup()
    _L0_cond_in = {k: v for k, v in _L0_cond_all.items() if k in ('weights',)}
    del _L0_cond_all

    def _L1_cond_setup():
        import jax, jax.numpy as jnp
        import numpy as np
        H, G, HD = (8, 4, 32)
        GSZ = H // G
        BLOCK = 16
        WINDOW = 128
        SCALE = 256.0 ** (-0.5)
        EPS = 1e-06
        THETA = 10000.0
        B, T, D = (16, 4, 256)
        NBLK = 257

        def _rms(x, scale):
            var = jnp.mean(x * x, axis=-1, keepdims=True)
            return x * jax.lax.rsqrt(var + EPS) * (1.0 + scale)

        def _rope(x, pos):
            half = HD // 2
            inv = 1.0 / THETA ** (jnp.arange(half, dtype=jnp.float32) / half)
            ang = pos[:, :, None].astype(jnp.float32) * inv
            cos = jnp.cos(ang)[:, None, :, :]
            sin = jnp.sin(ang)[:, None, :, :]
            x1, x2 = (x[..., :half], x[..., half:])
            return jnp.concatenate([x1 * cos - x2 * sin, x2 * cos + x1 * sin], axis=-1)
        key = jax.random.key(seed)
        ks = jax.random.split(key, 10)
        inv_d = 1.0 / np.sqrt(D)
        return {'x': jax.random.normal(ks[0], (B, T, D), jnp.float32), 'Wq': jax.random.normal(ks[1], (H * HD, D), jnp.float32) * inv_d, 'Wk': jax.random.normal(ks[2], (G * HD, D), jnp.float32) * inv_d, 'Wv': jax.random.normal(ks[3], (G * HD, D), jnp.float32) * inv_d, 'Wo': jax.random.normal(ks[4], (D, H * HD), jnp.float32) * inv_d, 'q_norm_scale': jax.random.normal(ks[5], (HD,), jnp.float32) * 0.02, 'k_norm_scale': jax.random.normal(ks[6], (HD,), jnp.float32) * 0.02, 'k_blocks': jax.random.normal(ks[7], (B * NBLK, G, BLOCK, HD), jnp.float32), 'v_blocks': jax.random.normal(ks[8], (B * NBLK, G, BLOCK, HD), jnp.float32), 'block_tables': jnp.arange(B * NBLK, dtype=jnp.int32).reshape(B, NBLK), 'kv_lens': jax.random.randint(ks[9], (B,), 0, 512, dtype=jnp.int32)}
    _L1_cond_all = _L1_cond_setup()
    _L1_cond_in = {k: v for k, v in _L1_cond_all.items() if k in ('Wq', 'Wk', 'Wv', 'Wo', 'q_norm_scale', 'k_norm_scale', 'k_blocks', 'v_blocks')}
    del _L1_cond_all
    return {'x': x, 'itok_B_1_198': itok_B_1_198, 'itok_Bx257_0_4111': itok_Bx257_0_4111, 'itok_B_37_3939': itok_B_37_3939, 'L0_cond_weights': _L0_cond_in['weights'], 'L1_cond_Wq': _L1_cond_in['Wq'], 'L1_cond_Wk': _L1_cond_in['Wk'], 'L1_cond_Wv': _L1_cond_in['Wv'], 'L1_cond_Wo': _L1_cond_in['Wo'], 'L1_cond_q_norm_scale': _L1_cond_in['q_norm_scale'], 'L1_cond_k_norm_scale': _L1_cond_in['k_norm_scale'], 'L1_cond_k_blocks': _L1_cond_in['k_blocks'], 'L1_cond_v_blocks': _L1_cond_in['v_blocks']}

def reference(x, itok_B_1_198, itok_Bx257_0_4111, itok_B_37_3939, L0_cond_weights, L1_cond_Wq, L1_cond_Wk, L1_cond_Wv, L1_cond_Wo, L1_cond_q_norm_scale, L1_cond_k_norm_scale, L1_cond_k_blocks, L1_cond_v_blocks):
    import jax
    import jax.numpy as jnp

    def _L0_cond_ref(x, conditions, weights):
        import jax, jax.numpy as jnp
        import numpy as np
        B, C, T = (128, 32, 256)
        S, D = (200, 32)
        w = weights[conditions]
        return jnp.einsum('bct,bcd->bdt', x, w)

    def _L1_cond_ref(x, Wq, Wk, Wv, Wo, q_norm_scale, k_norm_scale, k_blocks, v_blocks, block_tables, kv_lens):
        import jax, jax.numpy as jnp
        import numpy as np
        H, G, HD = (8, 4, 32)
        GSZ = H // G
        BLOCK = 16
        WINDOW = 128
        SCALE = 256.0 ** (-0.5)
        EPS = 1e-06
        THETA = 10000.0
        B, T, D = (16, 4, 256)
        NBLK = 257

        def _rms(x, scale):
            var = jnp.mean(x * x, axis=-1, keepdims=True)
            return x * jax.lax.rsqrt(var + EPS) * (1.0 + scale)

        def _rope(x, pos):
            half = HD // 2
            inv = 1.0 / THETA ** (jnp.arange(half, dtype=jnp.float32) / half)
            ang = pos[:, :, None].astype(jnp.float32) * inv
            cos = jnp.cos(ang)[:, None, :, :]
            sin = jnp.sin(ang)[:, None, :, :]
            x1, x2 = (x[..., :half], x[..., half:])
            return jnp.concatenate([x1 * cos - x2 * sin, x2 * cos + x1 * sin], axis=-1)
        Bx, Tx, _ = x.shape
        q = jnp.einsum('btd,od->bto', x, Wq).reshape(Bx, Tx, H, HD).transpose(0, 2, 1, 3)
        k = jnp.einsum('btd,od->bto', x, Wk).reshape(Bx, Tx, G, HD).transpose(0, 2, 1, 3)
        v = jnp.einsum('btd,od->bto', x, Wv).reshape(Bx, Tx, G, HD).transpose(0, 2, 1, 3)
        q = _rms(q, q_norm_scale)
        k = _rms(k, k_norm_scale)
        pos = kv_lens[:, None] + jnp.arange(Tx, dtype=jnp.int32)
        q = _rope(q, pos)
        k = _rope(k, pos)
        slot = pos // BLOCK
        off = pos % BLOCK
        blk = jnp.take_along_axis(block_tables, slot, axis=1)
        k_blocks = k_blocks.at[blk, :, off, :].set(k.transpose(0, 2, 1, 3))
        v_blocks = v_blocks.at[blk, :, off, :].set(v.transpose(0, 2, 1, 3))
        k_all = k_blocks[block_tables].transpose(0, 2, 1, 3, 4).reshape(Bx, G, -1, HD)
        v_all = v_blocks[block_tables].transpose(0, 2, 1, 3, 4).reshape(Bx, G, -1, HD)
        S = k_all.shape[2]
        qg = q.reshape(Bx, G, GSZ, Tx, HD)
        scores = jnp.einsum('bghtd,bgsd->bghts', qg, k_all) * SCALE
        kpos = jnp.arange(S, dtype=jnp.int32)
        allowed = (kpos[None, None, :] <= pos[:, :, None]) & (kpos[None, None, :] > pos[:, :, None] - WINDOW)
        scores = jnp.where(allowed[:, None, None, :, :], scores, -jnp.inf)
        p = jax.nn.softmax(scores, axis=-1)
        o = jnp.einsum('bghts,bgsd->bghtd', p, v_all).reshape(Bx, H, Tx, HD)
        o = o.transpose(0, 2, 1, 3).reshape(Bx, Tx, H * HD)
        return jnp.einsum('bto,do->btd', o, Wo)
    x = x + _L0_cond_ref(x, itok_B_1_198, L0_cond_weights)
    x = x + _L1_cond_ref(x, L1_cond_Wq, L1_cond_Wk, L1_cond_Wv, L1_cond_Wo, L1_cond_q_norm_scale, L1_cond_k_norm_scale, L1_cond_k_blocks, L1_cond_v_blocks, itok_Bx257_0_4111, itok_B_37_3939)
    return x

_drawn_inputs = setup_inputs


def setup_inputs(seed=0):
    import zlib

    import numpy as np

    out = dict(_drawn_inputs(seed))
    spreads = {}
    factors = {'L1_cond_q_norm_scale': 8.0,
     'L1_cond_k_norm_scale': 64.0,
     'L1_cond_k_blocks': 3.398,
     'L1_cond_Wk': 2.977}
    for name, (base, spread) in spreads.items():
        noise = np.random.default_rng([zlib.crc32(name.encode()), seed]).standard_normal(out[name].shape)
        drawn = base * np.exp(spread * noise) if base else spread * noise
        out[name] = jnp.asarray(drawn.astype(out[name].dtype))
    for name, factor in factors.items():
        out[name] = (out[name] * factor).astype(out[name].dtype)
    return out
```

```python
import numpy as np
import concourse.bass as bass
from concourse import mybir
from contextlib import ExitStack

F32 = mybir.dt.float32
I32 = mybir.dt.int32
ALU = mybir.AluOpType
ACT = mybir.ActivationFunctionType
AX = mybir.AxisListType

P = 128
B, T, D = 128, 32, 256
H, G, HD = 8, 4, 32
H2 = H // G
HALF = HD // 2
BLOCK, WINDOW = 16, 128
NBLK = 257
CACHE = 16 * NBLK
CONDS = 200
EPS = 1e-6
THETA = 10000.0
SCALE = 256.0 ** (-0.5)
BW = G * BLOCK * HD
TOK = G * HD

TPS = P // T
NT = B // TPS
NG = NT // 2
SLOTS = 11
PADDED = 16
BACK = WINDOW // BLOCK
WR = 3
KEYS = SLOTS * BLOCK
CH = KEYS // 2
NW = WR * B
SKIP = 65536.0
BIG = float(2.0 ** 100)
HUGE = 3.0e38
TWO_PI_A, TWO_PI_B = 6.28125, 0.0019350051879882812
TWO_PI_C = float(2 * np.pi - TWO_PI_A - TWO_PI_B)
ROUND = float(1.5 * 2 ** 23)
PI_IN = 3.1415925


def constants():
    p = np.arange(P)
    key_slot, key_off = np.arange(KEYS) // BLOCK, np.arange(KEYS) % BLOCK
    dist = (BLOCK * (key_slot - BACK) + key_off).astype(np.float64)
    row = lambda a: np.tile(np.asarray(a, np.float64).reshape(1, -1), (P, 1))
    parts = {
        "ident": np.eye(P),
        "ones": np.ones((P, P)),
        "same_quadrant": (p[:, None] // T == p[None, :] // T),
        "token_of_seq": (p[:, None] % TPS == p[None, :] // T),
        "seq_of_slot": (p[:, None] % (2 * TPS) == row(np.arange(8))[:1] % 2 * TPS + row(np.arange(8))[:1] // 2),
        "in_group": (p[:, None] // 8 == np.arange(NG)[None, :]),
        "in_tile": (p[:, None] // TPS == np.arange(NT)[None, :]),
        "eye_t": (p[:, None] % T == np.arange(HD)[None, :]),
        "t": (p % T)[:, None],
        "eps": np.full((P, 1), EPS),
        "slot": row(np.arange(SLOTS)),
        "column": row(np.arange(NBLK)),
        "inv_freq": row(1.0 / np.float32(THETA) ** (np.arange(HALF, dtype=np.float32) / np.float32(HALF))),
        "off": row(np.arange(BLOCK)),
        "first_token": row(T * np.arange(B) + 1),
        "dist": row(dist * BIG),
        "neg_dist": row(-dist * BIG),
        "writer": row(np.arange(NW) + 1),
    }
    at, n = {}, 0
    for name, a in parts.items():
        at[name] = (n, a.shape[1])
        n += a.shape[1]
    return np.concatenate([a.astype(np.float32) for a in parts.values()], axis=1), at


def build(nc, at, x, cond, table, kv_lens, l0_w, wq, wk, wv, wo, q_scale, k_scale, k_blocks, v_blocks, consts, out):
    with ExitStack() as ctx:
        def sb(name, cols, dt=F32):
            return ctx.enter_context(nc.sbuf_tensor(name, [P, cols], dt))

        def sem(name):
            return ctx.enter_context(nc.semaphore(name))

        l0_rows = nc.dram_tensor("l0_rows", (B, T * HD), F32, kind="Internal").ap()
        new_kv = nc.dram_tensor("new_kv", (B * T, 2 * TOK), F32, kind="Internal").ap()
        upd = [nc.dram_tensor(n, (NW, BW), F32, kind="Internal").ap() for n in ("updated_k", "updated_v")]

        X = sb("x_res", NT * D)
        Q = sb("q_rows", NT * D)
        CST = sb("consts", consts.shape[1])
        WO_T = sb("wo_t", H2 * D)
        RSTD_Q = sb("rstd_q", NT * H)
        small = sb("small", 520)
        ints = sb("ints", 120, I32)
        ARENA = sb("arena", 31744)

        def c(name, a=0, b=None):
            s, n = at[name]
            return CST[:, s + a:s + (n if b is None else b)]

        x3 = X[:, :].rearrange("p (j d) -> p j d", d=D)
        q3 = Q[:, :].rearrange("p (j d) -> p j d", d=D)
        used = [0]

        def cut(n):
            s = used[0]
            used[0] += n
            return small[:, s:s + n]

        kv_f, a_f, r_f = cut(1), cut(1), cut(1)
        slot_no, blk = cut(SLOTS), cut(PADDED)
        by_tile = cut(2 * NT)
        pos, hi, lo = cut(NT), cut(NT), cut(NT)
        qk_gain = cut(4 * HD)
        match, miss = cut(SLOTS), cut(SLOTS)
        ss, sd = cut(HD), cut(HD)
        won = small[:, 460:508]
        assert used[0] <= 460
        n_cols = [0]

        def icut(n):
            s = n_cols[0]
            n_cols[0] += n
            return ints[:, s:s + n]

        kv_i, a_i, cond_i = icut(1), icut(1), icut(1)
        base_idx, win_idx = icut(WR), icut(WR * BLOCK)
        idx_cache, idx_upd = icut(NG), icut(NG)

        def region(s, n):
            return ARENA[:, s:s + n]

        BASE = [[region(4096 * j + 2048 * kv, BW) for kv in range(2)] for j in range(WR)]
        W_RAW = region(0, 1536).rearrange("p (o d) -> p o d", d=D)
        TBL_I = ARENA[:, 1536:1536 + NBLK].bitcast(I32)
        TBL = region(1536 + NBLK, NBLK)
        ANG = [region(2050 + 512 * i, NT * HALF) for i in range(3)]
        EQ = region(3586, WR * NW)
        JUNK = region(4738, NW)
        ROWS = region(5122, 512)
        CAND = region(5634, WR * BLOCK * B).rearrange("p (o j b) -> p o j b", j=WR, b=B)
        DIAG = region(11778, 512)
        MATCHES = region(5634, SLOTS * NW)
        LHS = [region(5634 + 4224 + P * i, P) for i in range(2)]
        R0 = 12288
        MERGE = [region(R0 + 4096 * j, BLOCK * 2 * TOK) for j in range(WR)]
        ROW = region(R0, NT * 2 * TOK).rearrange("p (j c) -> p j c", c=2 * TOK)
        A1 = R0 + 8192
        L0_W = region(A1, NT * HD).rearrange("p (j d) -> p j d", d=HD)
        W_DIAG = [region(A1 + 1024 + P * i, P) for i in range(2)]
        W_QKV = region(A1 + 1280, 2 * 512).rearrange("p (c n) -> p c n", c=2)
        X1S = [region(A1 + 2304 + D * i, D) for i in range(2)]
        X1T = [region(A1 + 2816 + D * i, D) for i in range(2)]
        SQ, TA, TB = (region(24576 + 1024 * i, 1024) for i in range(3))
        TABS = [region(27648 + 1024 * i, NT * HD).rearrange("p (j d) -> p j d", d=HD) for i in range(4)]
        COS_Q, SIN_Q, COS_K, SIN_K = TABS

        KG = [region(2048 * i, BW) for i in range(2)]
        VG = [region(4096 + 2048 * i, BW) for i in range(2)]
        KT = [region(8192 + 2048 * i, BW) for i in range(2)]
        VT = [region(12288 + 2048 * i, BW) for i in range(2)]
        PR = [region(16384 + H * KEYS * i, H * KEYS).rearrange("p (h k) -> p h k", k=KEYS) for i in range(2)]
        PT = [region(19200 + 2048 * i, 2048) for i in range(2)]
        VR = [region(23296 + 1024 * i, 1024) for i in range(2)]
        QD = [region(25344 + 1024 * i, 1024).rearrange("p (h n) -> p h n", n=P) for i in range(2)]
        AT = [region(27392 + D * i, D) for i in range(2)]
        RB = region(27904, D)
        Y = [region(28160 + D * i, D) for i in range(2)]
        R32 = [region(28672 + D * i, D) for i in range(2)]
        QS = [region(29184 + D * i, D) for i in range(2)]
        MASK = [region(29696 + KEYS * i, KEYS) for i in range(2)]
        LOWER = region(30048, KEYS)
        NMAX = [region(30224 + H * i, H) for i in range(2)]
        SUMS = [region(30240 + H * i, H) for i in range(2)]

        PS = [ctx.enter_context(nc.psum_tensor(f"bank{i}", [P, 512], F32)) for i in range(8)]

        consts_in, ints_in, w_in, gain_in, l0_got, l0_kept, l0_in = (sem(n) for n in (
            "consts_in", "ints_in", "w_in", "gain_in", "l0_got", "l0_kept", "l0_in"))
        x_in, cond_in = sem("x_in"), sem("cond_in")
        dve_step, pool_step, act_step = sem("dve_step"), sem("pool_step"), sem("act_step")
        spread_rhs, spread_ps, diag_set, rows_ps, rows_set = (sem(n) for n in (
            "spread_rhs", "spread_ps", "diag_set", "rows_ps", "rows_set"))
        cand_set, win_set, base_set, lhs_set, idx_ps, idx_set = (sem(n) for n in (
            "cand_set", "win_set", "base_set", "lhs_set", "idx_ps", "idx_set"))
        turned, kept_w, angles, sines, cosines, gains, tables = (sem(n) for n in (
            "turned", "kept_w", "angles", "sines", "cosines", "gains", "tables"))
        l0_w_set, w_diag_set, l0_done, x1_set, x1_turned, x1t_set, qkv_done, kv_kept = (sem(n) for n in (
            "l0_w_set", "w_diag_set", "l0_done", "x1_set", "x1_turned", "x1t_set", "qkv_done", "kv_kept"))
        k_squared, k_crossed, k_summed, k_root, k_roped, kv_stored = (sem(n) for n in (
            "k_squared", "k_crossed", "k_summed", "k_root", "k_roped", "kv_stored"))
        base_in = [sem(f"base_in{j}") for j in range(WR)]
        won_in = [sem(f"won_in{j}") for j in range(WR)]
        laid_k, laid_v, merged_k, merged_v, upd_stored = (sem(n) for n in (
            "laid_k", "laid_v", "merged_k", "merged_v", "upd_stored"))
        q_squared, q_summed, q_root, q_rstd = (sem(n) for n in ("q_squared", "q_summed", "q_root", "q_rstd"))
        cleared = sem("cleared")
        k_in = [sem(f"k_in{i}") for i in range(2)]
        v_in = [sem(f"v_in{i}") for i in range(2)]
        kt_set, vt_set, q_scaled, qd_set, mask_set = (sem(n) for n in (
            "kt_set", "vt_set", "q_scaled", "qd_set", "mask_set"))
        scored, masked, probs, p_turned, p_kept, v_turned, v_kept = (sem(n) for n in (
            "scored", "masked", "probs", "p_turned", "p_kept", "v_turned", "v_kept"))
        r_set, r_spread, r_kept, summed_o, o_scaled, y_done, y_set = (sem(n) for n in (
            "r_set", "r_spread", "r_kept", "summed_o", "o_scaled", "y_done", "y_set"))
        y_sent = [sem(f"y_sent{i}") for i in range(2)]

        KC, KN = 4, NT // 4
        QC, QN = 8, NT // 8

        block = ctx.enter_context(nc.Block())

        @block.sync
        def _(sp):
            sp.dma_start(kv_i, kv_lens.rearrange("(b o) -> b o", o=1)).then_inc(ints_in, 16)
            sp.dma_start(TBL_I, table).then_inc(ints_in, 16)
            sp.dma_start(CST[:, :], consts).then_inc(consts_in, 16)
            sp.dma_start(W_RAW[:, 0:2, :], wq.rearrange("(o p) d -> p o d", p=P)).then_inc(w_in, 16)
            sp.dma_start(W_RAW[:, 2, :], wk).then_inc(w_in, 16)
            sp.dma_start(W_RAW[:, 3, :], wv).then_inc(w_in, 16)
            for o in range(2):
                for e in range(H2):
                    sp.dma_start(W_RAW[:, 4 + o, P * e:P * (e + 1)].rearrange("p (g d) -> p g d", d=HD),
                                 wo[P * o:P * (o + 1), :].rearrange("p (g e d) -> p e g d", e=H2, d=HD)[:, e]).then_inc(w_in, 16)
            sp.dma_start(qk_gain[:, 0:HD], q_scale.rearrange("(o d) -> o d", o=1).to_broadcast([P, HD])).then_inc(gain_in, 16)
            sp.dma_start(qk_gain[:, 2 * HD:3 * HD], k_scale.rearrange("(o d) -> o d", o=1).to_broadcast([P, HD])).then_inc(gain_in, 16)
            sp.wait_ge(l0_got, 16)
            sp.dma_start(l0_rows, Q[:, 0:T * HD]).then_inc(l0_kept, 16)
            x_tiles = x.rearrange("(j s) c t -> (s c) j t", s=TPS)
            for n in range(2):
                sp.dma_start(x3[:, 16 * n:16 * n + 16, :], x_tiles[:, 16 * n:16 * n + 16, :]).then_inc(x_in, 16)
            sp.wait_ge(l0_kept, 16)
            sp.dma_start(L0_W, l0_rows.rearrange("(j s) (c d) -> (s c) j d", s=TPS, d=HD)).then_inc(l0_in, 16)
            for n in range(KC):
                sp.wait_ge(k_roped, n + 1)
                sp.dma_start(new_kv.rearrange("(j p) c -> p j c", p=P)[:, KN * n:KN * (n + 1), :],
                             ROW[:, KN * n:KN * (n + 1), :]).then_inc(kv_stored, 16)
            for j in range(WR):
                sp.wait_ge(merged_k, j + 1)
                sp.dma_start(upd[0][P * j:P * (j + 1), :], BASE[j][0]).then_inc(upd_stored, 16)
                sp.wait_ge(merged_v, j + 1)
                sp.dma_start(upd[1][P * j:P * (j + 1), :], BASE[j][1]).then_inc(upd_stored, 16)
            out_tiles = out.rearrange("(j s) c t -> j (s c) t", s=TPS)
            with sp.Fori(0, NG) as g:
                for b2 in range(2):
                    sp.wait_ge(y_set, 2 * g + b2 + 1)
                    sp.dma_start(out_tiles[bass.ds(2 * g + b2, 1)].rearrange("o p t -> p (o t)"),
                                 Y[b2]).then_inc(y_sent[b2], 16)
            for b2 in range(2):
                sp.wait_ge(y_sent[b2], 16 * NG)

        @block.gpsimd
        def _(pool):
            steps = [0]

            def link(ins):
                steps[0] += 1
                ins.then_inc(pool_step, 1)
                pool.wait_ge(pool_step, steps[0])

            pool.dma_start(cond_i, cond.rearrange("(b o) -> b o", o=1)).then_inc(cond_in, 16)
            pool.wait_ge(cond_in, 16)
            pool.indirect_dma_start(Q[:, 0:T * HD], None, l0_w.rearrange("s c d -> s (c d)"),
                                    bass.IndirectOffsetOnAxis(cond_i, 0), bounds_check=CONDS - 1,
                                    oob_is_err=False).then_inc(l0_got, 16)
            pool.wait_ge(l0_in, 16)
            pool.wait_ge(consts_in, 16)
            pool.tensor_tensor(L0_W, L0_W, c("eye_t").unsqueeze(1).to_broadcast([P, NT, HD]), ALU.add).then_inc(l0_w_set, 1)
            pool.wait_ge(l0_w_set, 1)

            def w_diag(j, slot):
                pool.tensor_tensor(W_DIAG[slot].rearrange("p (s d) -> p s d", s=TPS),
                                   L0_W[:, bass.ds(j, 1), :].to_broadcast([P, TPS, HD]),
                                   c("same_quadrant").rearrange("p (s d) -> p s d", s=TPS),
                                   ALU.mult).then_inc(w_diag_set, 1)

            w_diag(0, 0)
            w_diag(1, 1)
            pool.wait_ge(rows_set, 1)
            per_off = [P, BLOCK, B]
            r_row = ROWS[:, NW:NW + B].unsqueeze(1).to_broadcast(per_off)
            off_col = c("off").unsqueeze(2).to_broadcast(per_off)
            token = c("first_token").unsqueeze(1).to_broadcast(per_off)
            link(pool.tensor_tensor(CAND[:, :, 2, :], off_col, r_row, ALU.subtract))
            link(pool.tensor_tensor(CAND[:, :, 1, :], CAND[:, :, 2, :], token, ALU.add))
            link(pool.tensor_scalar(CAND[:, :, 0, :], CAND[:, :, 2, :], 0.0, None, ALU.is_ge))
            link(pool.tensor_tensor(CAND[:, :, 0, :], CAND[:, :, 0, :], CAND[:, :, 1, :], ALU.mult))
            link(pool.tensor_scalar(CAND[:, :, 2, :], CAND[:, :, 2, :], 0.0, None, ALU.is_lt))
            link(pool.tensor_scalar(CAND[:, :, 1, :], CAND[:, :, 1, :], float(2 * BLOCK), None, ALU.add))
            link(pool.tensor_tensor(CAND[:, :, 2, :], CAND[:, :, 2, :], CAND[:, :, 1, :], ALU.mult))
            pool.tensor_scalar(CAND[:, :, 1, :], CAND[:, :, 1, :], float(BLOCK), None, ALU.subtract).then_inc(cand_set, 1)
            pool.wait_ge(cosines, 1)
            pool.wait_ge(gains, 1)
            sin, cos = (a.rearrange("p (j f) -> p j f", f=HALF) for a in (ANG[1], ANG[2]))
            for tabs, g0 in (((COS_K, SIN_K), 2 * HD), ((COS_Q, SIN_Q), 0)):
                gain = lambda a: qk_gain[:, g0 + a:g0 + a + HALF].unsqueeze(1).to_broadcast([P, NT, HALF])
                for tab, half, trig, g in ((0, 0, cos, 0), (0, 1, cos, HALF), (1, 0, sin, HD + HALF), (1, 1, sin, 0)):
                    pool.tensor_tensor(tabs[tab][:, :, HALF * half:HALF * (half + 1)], trig, gain(g),
                                       ALU.mult).then_inc(tables, 1)
            with pool.Fori(1, NG) as i:
                for u in range(2):
                    pool.wait_ge(l0_done, 2 * i + u - 1)
                    w_diag(2 * i + u, u)
            pool.wait_ge(tables, 8)
            with pool.Fori(0, KC) as n:
                tiles = bass.ds(KN * n, KN)
                k = ROW[:, tiles, 0:TOK]
                pool.wait_ge(kv_kept, KN * (n + 1))
                pool.tensor_tensor(SQ.rearrange("p (j c) -> p j c", c=TOK), k, k, ALU.mult).then_inc(k_squared, 1)
                for half in range(2):
                    for g in range(G):
                        src = ROW[:, tiles, HD * g + HALF * (1 - half):HD * g + HALF * (2 - half)]
                        dst = TB.rearrange("p (j c) -> p j c", c=TOK)[:, :, HD * g + HALF * half:HD * g + HALF * (half + 1)]
                        pool.tensor_tensor(dst, src, SIN_K[:, tiles, HALF * half:HALF * (half + 1)], ALU.mult).then_inc(k_crossed, 1)
                pool.wait_ge(k_roped, n + 1)
            pool.wait_ge(win_set, 1)
            pool.wait_ge(base_set, 1)
            pool.wait_ge(idx_set, 2)
            for j in range(WR):
                for kv, cache in enumerate((k_blocks, v_blocks)):
                    pool.indirect_dma_start(BASE[j][kv], None, cache.rearrange("n g o d -> n (g o d)"),
                                            bass.IndirectOffsetOnAxis(base_idx[:, j:j + 1], 0),
                                            bounds_check=CACHE - 1, oob_is_err=False).then_inc(base_in[j], 16)
            pool.wait_ge(kv_stored, 16 * KC)
            for j in range(WR):
                pool.wait_ge(laid_k, j + 1)
                pool.wait_ge(laid_v, j + 1)
                for o in range(BLOCK):
                    pool.indirect_dma_start(MERGE[j][:, 2 * TOK * o:2 * TOK * (o + 1)], None, new_kv,
                                            bass.IndirectOffsetOnAxis(win_idx[:, BLOCK * j + o:BLOCK * j + o + 1], 0),
                                            bounds_check=B * T - 1, oob_is_err=False).then_inc(won_in[j], 16)
            pool.wait_ge(upd_stored, 16 * 2 * WR)
            for i in range(2):
                pool.memset(KG[i], 0.0).then_inc(cleared, 1)
                pool.memset(VG[i], 0.0).then_inc(cleared, 1)
            pool.wait_ge(cleared, 4)

            def gather(g):
                for buf, got, cache in ((KG, k_in, k_blocks), (VG, v_in, v_blocks)):
                    pool.indirect_dma_start(buf[g % 2], None, cache.rearrange("n g o d -> n (g o d)"),
                                            bass.IndirectOffsetOnAxis(idx_cache[:, g:g + 1], 0),
                                            bounds_check=CACHE - 1, oob_is_err=False).then_inc(got[g % 2], 16)
                for buf, got, new in ((KG, k_in, upd[0]), (VG, v_in, upd[1])):
                    pool.wait_ge(got[g % 2], 32 * (g // 2) + 16)
                    pool.indirect_dma_start(buf[g % 2], None, new,
                                            bass.IndirectOffsetOnAxis(idx_upd[:, g:g + 1], 0),
                                            bounds_check=NW - 1, oob_is_err=False).then_inc(got[g % 2], 16)

            gather(0)
            gather(1)
            pool.wait_ge(q_rstd, QC)
            for n in range(NT):
                if n >= 2:
                    pool.wait_ge(qd_set, n - 1)
                pool.tensor_tensor(QS[n % 2].rearrange("p (h d) -> p h d", d=HD),
                                   q3[:, n, :].rearrange("p (h d) -> p h d", d=HD),
                                   RSTD_Q[:, H * n:H * (n + 1)].unsqueeze(2).to_broadcast([P, H, HD]),
                                   ALU.mult).then_inc(q_scaled, 1)
                if n % 2 == 1 and n // 2 + 2 < NG:
                    pool.wait_ge(kt_set, n // 2 + 1)
                    pool.wait_ge(vt_set, n // 2 + 1)
                    gather(n // 2 + 2)

        @block.vector
        def _(dve):
            steps = [0]

            def link(ins):
                steps[0] += 1
                ins.then_inc(dve_step, 1)
                dve.wait_ge(dve_step, steps[0])

            dve.wait_ge(ints_in, 32)
            link(dve.tensor_scalar(a_i, kv_i, 4, None, ALU.arith_shift_right))
            dve.tensor_copy(kv_f, kv_i).then_inc(dve_step, 1)
            dve.tensor_copy(TBL, TBL_I).then_inc(dve_step, 1)
            steps[0] += 2
            link(dve.tensor_copy(a_f, a_i))
            dve.wait_ge(consts_in, 16)
            dve.tensor_scalar(by_tile[:, 0:NT], c("in_tile"), kv_f, None, ALU.mult).then_inc(spread_rhs, 1)
            dve.tensor_scalar(by_tile[:, NT:2 * NT], c("in_tile"), a_f, None, ALU.mult).then_inc(spread_rhs, 1)
            link(dve.scalar_tensor_tensor(r_f, a_f, -float(BLOCK), kv_f, ALU.mult, ALU.add))
            link(dve.tensor_scalar(slot_no, c("slot"), a_f, -float(BACK), ALU.add, ALU.add))
            link(dve.tensor_scalar(slot_no, slot_no, 0.0, float(NBLK - 1), ALU.max, ALU.min))
            link(dve.memset(blk, SKIP))
            for s in range(SLOTS):
                dve.scalar_tensor_tensor(MATCHES[:, NBLK * s:NBLK * (s + 1)], c("column"), slot_no[:, s:s + 1], TBL,
                                         ALU.is_equal, ALU.mult, accum_out=blk[:, s:s + 1]).then_inc(dve_step, 1)
            steps[0] += SLOTS
            dve.wait_ge(dve_step, steps[0])
            for j in range(WR):
                dve.tensor_scalar(DIAG[:, B * j:B * (j + 1)], c("ident"), blk[:, BACK + j:BACK + j + 1], None,
                                  ALU.mult).then_inc(diag_set, 1)
            dve.tensor_scalar(DIAG[:, NW:NW + B], c("ident"), r_f, None, ALU.mult).then_inc(diag_set, 1)
            dve.tensor_copy(base_idx, blk[:, BACK:BACK + WR]).then_inc(base_set, 1)
            dve.wait_ge(spread_ps, 1)
            link(dve.tensor_scalar(pos, PS[6][:, 0:NT], c("t"), None, ALU.add))
            link(dve.scalar_tensor_tensor(hi, PS[6][:, NT:2 * NT], -float(BLOCK), pos, ALU.mult, ALU.add))
            link(dve.tensor_scalar(lo, hi, -float(WINDOW - 1), None, ALU.add))
            link(dve.scalar_tensor_tensor(lo, PS[6][:, NT:2 * NT], -float(BLOCK), lo, ALU.mult, ALU.max))
            link(dve.tensor_scalar(hi, hi, BIG, None, ALU.mult))
            link(dve.tensor_scalar(lo, lo, BIG, None, ALU.mult))
            a0, a1, a2 = ANG
            grid = lambda a: a.rearrange("p (j f) -> p j f", f=HALF)
            link(dve.tensor_tensor(grid(a0), pos.unsqueeze(2).to_broadcast([P, NT, HALF]),
                                   c("inv_freq").unsqueeze(1).to_broadcast([P, NT, HALF]), ALU.mult))
            link(dve.tensor_scalar(a1, a0, float(1 / (2 * np.pi)), ROUND, ALU.mult, ALU.add))
            link(dve.tensor_scalar(a1, a1, ROUND, None, ALU.subtract))
            for part in (TWO_PI_A, TWO_PI_B, TWO_PI_C):
                link(dve.scalar_tensor_tensor(a0, a1, -part, a0, ALU.mult, ALU.add))
            dve.tensor_scalar(a0, a0, PI_IN, -PI_IN, ALU.min, ALU.max).then_inc(angles, 1)
            dve.wait_ge(gain_in, 32)
            link(dve.tensor_scalar(qk_gain[:, 0:HD], qk_gain[:, 0:HD], 1.0, -SCALE, ALU.add, ALU.mult))
            link(dve.tensor_scalar(qk_gain[:, HD:2 * HD], qk_gain[:, 0:HD], -1.0, None, ALU.mult))
            link(dve.tensor_scalar(qk_gain[:, 2 * HD:3 * HD], qk_gain[:, 2 * HD:3 * HD], 1.0, None, ALU.add))
            dve.tensor_scalar(qk_gain[:, 3 * HD:4 * HD], qk_gain[:, 2 * HD:3 * HD], -1.0, None, ALU.mult).then_inc(gains, 1)
            dve.wait_ge(sines, 2)
            link(dve.tensor_tensor(a2, a2, a2, ALU.mult))
            dve.tensor_scalar(a2, a2, -2.0, 1.0, ALU.mult, ALU.add).then_inc(cosines, 1)
            dve.wait_ge(rows_set, 1)
            for j in range(WR):
                dve.tensor_scalar(EQ[:, NW * j:NW * (j + 1)], ROWS[:, 0:NW], blk[:, BACK + j:BACK + j + 1], None,
                                  ALU.is_equal).then_inc(dve_step, 1)
            steps[0] += WR
            dve.wait_ge(dve_step, steps[0])
            dve.wait_ge(cand_set, 1)
            for j in range(WR):
                for o in range(BLOCK):
                    link(dve.tensor_tensor_reduce(
                        out=JUNK, in0=EQ[:, NW * j:NW * (j + 1)], in1=CAND[:, o, :, :].rearrange("p j b -> p (j b)"),
                        scale=1.0, scalar=0.0, op0=ALU.mult, op1=ALU.max,
                        accum_out=won[:, BLOCK * j + o:BLOCK * j + o + 1]))
            link(dve.tensor_scalar(JUNK[:, 0:WR * BLOCK], won, 0.0, SKIP, ALU.is_equal, ALU.mult))
            dve.scalar_tensor_tensor(win_idx, won, -1.0, JUNK[:, 0:WR * BLOCK], ALU.add, ALU.add).then_inc(win_set, 1)
            for s in range(SLOTS):
                dve.scalar_tensor_tensor(MATCHES[:, NW * s:NW * (s + 1)], ROWS[:, 0:NW], blk[:, s:s + 1], c("writer"),
                                         ALU.is_equal, ALU.mult).then_inc(dve_step, 1)
            steps[0] += SLOTS
            dve.wait_ge(dve_step, steps[0])
            link(dve.tensor_reduce(match, MATCHES.rearrange("p (s w) -> p s w", w=NW), AX.X, ALU.max))
            link(dve.tensor_scalar(miss, match, 0.0, SKIP, ALU.is_gt, ALU.mult))
            link(dve.tensor_copy(slot_no, blk[:, 0:SLOTS]))
            link(dve.tensor_tensor(blk[:, 0:SLOTS], blk[:, 0:SLOTS], miss, ALU.add))
            lhs = [a.rearrange("p (s k) -> p s k", k=PADDED) for a in LHS]
            place = c("seq_of_slot").unsqueeze(2).to_broadcast([P, 8, PADDED])
            link(dve.tensor_tensor(lhs[0], blk.unsqueeze(1).to_broadcast([P, 8, PADDED]), place, ALU.mult))
            link(dve.tensor_scalar(miss, match, 0.0, SKIP, ALU.is_equal, ALU.mult))
            link(dve.scalar_tensor_tensor(blk[:, 0:SLOTS], match, -1.0, miss, ALU.add, ALU.add))
            dve.tensor_tensor(lhs[1], blk.unsqueeze(1).to_broadcast([P, 8, PADDED]), place, ALU.mult).then_inc(lhs_set, 1)
            dve.wait_ge(idx_ps, 1)
            dve.tensor_copy(idx_cache, PS[6][:, 0:NG]).then_inc(idx_set, 1)
            dve.tensor_copy(idx_upd, PS[6][:, NG:2 * NG]).then_inc(idx_set, 1)

            base = steps[0]
            per = 2
            dve.wait_ge(tables, 8)
            with dve.Fori(0, KC) as n:
                tiles = bass.ds(KN * n, KN)
                ta, tb = (a.rearrange("p (j c) -> p j c", c=TOK) for a in (TA, TB))
                dve.wait_ge(k_squared, n + 1)
                dve.tensor_reduce(ss, SQ.rearrange("p (h d) -> p h d", d=HD), AX.X, ALU.add).then_inc(k_summed, 1)
                for g in range(G):
                    dve.tensor_tensor(ta[:, :, HD * g:HD * (g + 1)], ROW[:, tiles, HD * g:HD * (g + 1)],
                                      COS_K[:, tiles, :], ALU.mult).then_inc(dve_step, 1)
                dve.wait_ge(k_crossed, 8 * n + 8)
                dve.wait_ge(dve_step, base + 6 * n + 4)
                dve.tensor_tensor(TA, TA, TB, ALU.add).then_inc(dve_step, 1)
                dve.wait_ge(k_root, n + 1)
                dve.reciprocal(sd, sd).then_inc(dve_step, 1)
                dve.wait_ge(dve_step, base + 6 * n + 6)
                dve.tensor_tensor(ROW[:, tiles, 0:TOK].rearrange("p j (g d) -> p j g d", d=HD),
                                  TA.rearrange("p (j g d) -> p j g d", g=G, d=HD),
                                  sd.rearrange("p (j g) -> p j g", g=G).unsqueeze(3).to_broadcast([P, KN, G, HD]),
                                  ALU.mult).then_inc(k_roped, 1)
            steps[0] = base + 6 * KC

            dve.wait_ge(kv_stored, 16 * KC)
            for j in range(WR):
                dve.wait_ge(base_in[j], 32)
                dve.tensor_copy(MERGE[j].rearrange("p (o c) -> p o c", o=BLOCK)[:, :, TOK:2 * TOK]
                                .rearrange("p o (g d) -> p g o d", g=G),
                                BASE[j][1].rearrange("p (g o d) -> p g o d", g=G, o=BLOCK)).then_inc(laid_v, 1)
            base = steps[0]
            with dve.Fori(0, QC) as n:
                tiles = bass.ds(QN * n, QN)
                qt = q3[:, tiles, :].rearrange("p j (h d) -> p j h d", d=HD)
                ta, tb = (a.rearrange("p (j h d) -> p j h d", j=QN, h=H) for a in (TA, TB))
                wide = [P, QN, H, HD]
                dve.wait_ge(q_squared, n + 1)
                dve.tensor_reduce(ss, SQ.rearrange("p (h d) -> p h d", d=HD), AX.X, ALU.add).then_inc(q_summed, 1)
                dve.tensor_tensor(ta, qt, COS_Q[:, tiles, :].unsqueeze(2).to_broadcast(wide), ALU.mult).then_inc(dve_step, 1)
                for half in range(2):
                    dve.tensor_tensor(tb[:, :, :, HALF * half:HALF * (half + 1)],
                                      qt[:, :, :, HALF * (1 - half):HALF * (2 - half)],
                                      SIN_Q[:, tiles, HALF * half:HALF * (half + 1)].unsqueeze(2).to_broadcast([P, QN, H, HALF]),
                                      ALU.mult).then_inc(dve_step, 1)
                dve.wait_ge(dve_step, base + 4 * n + 3)
                dve.tensor_tensor(qt, ta, tb, ALU.add).then_inc(dve_step, 1)
                dve.wait_ge(q_root, n + 1)
                dve.reciprocal(RSTD_Q[:, bass.ds(QN * H * n, QN * H)], sd).then_inc(q_rstd, 1)
                dve.wait_ge(dve_step, base + 4 * n + 4)
            steps[0] = base + 4 * QC
            for j in range(WR):
                dve.wait_ge(won_in[j], 16 * BLOCK)
                dve.tensor_copy(BASE[j][1].rearrange("p (g o d) -> p g o d", g=G, o=BLOCK),
                                MERGE[j].rearrange("p (o c) -> p o c", o=BLOCK)[:, :, TOK:2 * TOK]
                                .rearrange("p o (g d) -> p g o d", g=G)).then_inc(merged_v, 1)

            dve.wait_ge(upd_stored, 16 * 2 * WR)
            for b2 in range(2):
                link(dve.memset(QD[b2], 0.0))

            def by_key(buf):
                return buf.rearrange("p (g k o) -> p g o k", g=G, o=BLOCK)

            def turn_k(g, p):
                dve.wait_ge(k_in[p], 16 * (g - p) + 32)
                dve.transpose(by_key(KT[p]), KG[p].rearrange("p (g o d) -> p g o d", g=G, d=HD)).then_inc(kt_set, 1)

            def turn_v(g, p):
                dve.wait_ge(v_in[p], 16 * (g - p) + 32)
                dve.transpose(by_key(VT[p]), VG[p].rearrange("p (g o d) -> p g o d", g=G, d=HD)).then_inc(vt_set, 1)

            unit = dve.alloc_register("units_scored")
            dve.reg_mov(unit, 0)

            def spread_q(n, b2):
                dve.wait_ge(q_scaled, n + 1)
                for rg in range(TPS):
                    ins = dve.transpose(QD[b2][T * rg:T * (rg + 1), :, T * rg:T * (rg + 1)],
                                        QS[b2][T * rg:T * (rg + 1), :].rearrange("p (h d) -> p h d", d=HD))
                ins.then_inc(qd_set, 1)

            def mask(n, b2):
                dve.tensor_scalar(LOWER, c("neg_dist"), lo[:, bass.ds(n, 1)], 0.0, ALU.add, ALU.max).then_inc(mask_set, 1)
                dve.wait_ge(mask_set, 2 * n + 1)
                dve.scalar_tensor_tensor(MASK[b2], c("dist"), hi[:, bass.ds(n, 1)], LOWER, ALU.subtract, ALU.max).then_inc(mask_set, 1)

            def lower(n, b2, g):
                dve.wait_ge(mask_set, 2 * n + 2)
                dve.reg_add(unit, unit, 1)
                dve.wait_ge(upd_stored, 16 * 2 * WR)
                dve.wait_ge(scored, unit)
                for h2 in range(H2):
                    h = H2 * g + h2
                    dve.tensor_tensor_reduce(out=PR[b2][:, h, :], in0=PS[g % 2][:, KEYS * h2:KEYS * (h2 + 1)],
                                             in1=MASK[b2], scale=1.0, scalar=HUGE, op0=ALU.add, op1=ALU.min,
                                             accum_out=NMAX[b2][:, h:h + 1]).then_inc(masked, 1)

            def invert(n, b2):
                dve.wait_ge(probs, 8 * n + 8)
                dve.reciprocal(R32[b2].rearrange("p (e g d) -> p e g d", e=H2, g=G),
                               SUMS[b2].rearrange("p (g e) -> p e g", e=H2).unsqueeze(3)
                               .to_broadcast([P, H2, G, HD])).then_inc(r_set, 1)

            def scale_o(n, b2):
                dve.wait_ge(summed_o, n + 1)
                dve.wait_ge(r_kept, n + 1)
                dve.tensor_tensor(AT[b2], PS[5][:, D * b2:D * (b2 + 1)], RB, ALU.mult).then_inc(o_scaled, 1)

            def add_res(n, b2, sent):
                dve.wait_ge(y_done, n + 1)
                if sent is not None:
                    dve.wait_ge(y_sent[b2], sent)
                dve.tensor_tensor(Y[b2], PS[7][:, D * b2:D * (b2 + 1)],
                                  X[:, bass.ds(D * n, D)], ALU.add).then_inc(y_set, 1)

            def tiles4(i, first=False, last=False):
                for m in range(4):
                    n, b2, p = 4 * i + m, m % 2, m // 2
                    g = 2 * i + p
                    lower(n, b2, 0)
                    if not (first and m < 2):
                        add_res(n - 2, b2, None if first and m < 4 else 16 * (2 * i + p - 1))
                    if not (last and m == 3):
                        spread_q(n + 1, 1 - b2)
                        mask(n + 1, 1 - b2)
                    lower(n, b2, 1)
                    if not (first and m == 0):
                        invert(n - 1, 1 - b2)
                    if not (last and p == 1):
                        (turn_k, turn_v)[b2](g + 1, 1 - p)
                    lower(n, b2, 2)
                    lower(n, b2, 3)
                    if not (first and m == 0):
                        scale_o(n - 1, 1 - b2)

            turn_k(0, 0)
            turn_v(0, 0)
            spread_q(0, 0)
            mask(0, 0)
            tiles4(0, first=True)
            with dve.Fori(1, NT // 4 - 1) as i:
                tiles4(i)
            tiles4(NT // 4 - 1, last=True)
            add_res(NT - 2, 0, 16 * (NG - 1))
            invert(NT - 1, 1)
            scale_o(NT - 1, 1)
            add_res(NT - 1, 1, 16 * (NG - 1))

        @block.scalar
        def _(act):
            for n in range(3):
                act.wait_ge(turned, n + 1)
                if n < 2:
                    act.activation(W_QKV[:, n, :], PS[n][:, :], ACT.Copy).then_inc(kept_w, 1)
                else:
                    act.activation(WO_T[:, :], PS[2][:, :], ACT.Copy).then_inc(kept_w, 1)
            act.wait_ge(rows_ps, 1)
            act.activation(ROWS, PS[7][:, :], ACT.Copy).then_inc(rows_set, 1)
            act.wait_ge(angles, 1)
            act.activation(ANG[1], ANG[0], ACT.Sin).then_inc(sines, 1)
            act.activation(ANG[2], ANG[0], ACT.Sin, scale=0.5).then_inc(sines, 1)

            def x1(j, slot):
                act.wait_ge(l0_done, j + 1)
                act.activation(X1S[slot], PS[slot][:, 0:D], ACT.Copy).then_inc(x1_set, 1)
                act.activation(X[:, bass.ds(D * j, D)], PS[slot][:, 0:D], ACT.Copy).then_inc(x1_set, 1)

            def turned_x1(j, slot):
                act.wait_ge(x1_turned, j + 1)
                act.activation(X1T[slot], PS[2 + slot][:, 0:D], ACT.Copy).then_inc(x1t_set, 1)

            def keep_qkv(j, slot):
                act.wait_ge(qkv_done, j + 1)
                act.activation(ROW[:, bass.ds(j, 1), :].rearrange("p o c -> p (o c)"), PS[4 + slot][:, D:2 * D], ACT.Copy).then_inc(kv_kept, 1)
                act.activation(Q[:, bass.ds(D * j, D)], PS[4 + slot][:, 0:D], ACT.Copy).then_inc(act_step, 1)

            def root(n, done, got):
                act.wait_ge(got, n + 1)
                act.activation(sd, ss, ACT.Sqrt, bias=c("eps"), scale=1.0 / HD).then_inc(done, 1)

            def chunk(k, last=False):
                for u in range(KN):
                    j, slot = KN * k + u, u % 2
                    turned_x1(j, slot)
                    if not (last and u == KN - 1):
                        x1(j + 1, 1 - slot)
                    keep_qkv(j, slot)

            act.wait_ge(l0_kept, 16)
            x1(0, 0)
            with act.Fori(0, KC - 1) as k:
                chunk(k)
            chunk(KC - 1, last=True)
            for n in range(KC):
                root(n, k_root, k_summed)
            act.wait_ge(kv_stored, 16 * KC)
            for j in range(WR):
                act.wait_ge(base_in[j], 32)
                act.activation(MERGE[j].rearrange("p (o c) -> p o c", o=BLOCK)[:, :, 0:TOK]
                               .rearrange("p o (g d) -> p g o d", g=G),
                               BASE[j][0].rearrange("p (g o d) -> p g o d", g=G, o=BLOCK), ACT.Copy).then_inc(laid_k, 1)
            act.wait_ge(act_step, NT)

            def square_q(n):
                act.activation(SQ, Q[:, bass.ds(QN * D * n, QN * D)], ACT.Square).then_inc(q_squared, 1)

            square_q(0)
            with act.Fori(0, QC - 1) as n:
                root(n, q_root, q_summed)
                square_q(n + 1)
            root(QC - 1, q_root, q_summed)
            for j in range(WR):
                act.wait_ge(won_in[j], 16 * BLOCK)
                act.activation(BASE[j][0].rearrange("p (g o d) -> p g o d", g=G, o=BLOCK),
                               MERGE[j].rearrange("p (o c) -> p o c", o=BLOCK)[:, :, 0:TOK]
                               .rearrange("p o (g d) -> p g o d", g=G), ACT.Copy).then_inc(merged_k, 1)

            def exps(n, b2, g):
                for h2 in range(H2):
                    h = H2 * g + h2
                    act.wait_ge(masked, 8 * n + h + 1)
                    act.activation(PR[b2][:, h, :], PR[b2][:, h, :], ACT.Exp, bias=NMAX[b2][:, h:h + 1], scale=-1.0,
                                   accum_out=SUMS[b2][:, h:h + 1]).then_inc(probs, 1)

            def keep_p(n, b2, g):
                act.wait_ge(p_turned, 4 * n + g + 1)
                act.activation(PT[b2][0:CH, 512 * g:512 * (g + 1)], PS[2 + g % 2][0:CH, :], ACT.Copy).then_inc(p_kept, 1)

            def keep_v(n, b2, ch):
                act.wait_ge(v_turned, 2 * n + ch + 1)
                act.activation(VR[b2][0:CH, 512 * ch:512 * (ch + 1)], PS[4][0:CH, :], ACT.Copy).then_inc(v_kept, 1)

            def keep_r(n):
                act.wait_ge(r_spread, n + 1)
                act.activation(RB, PS[6][:, 0:D], ACT.Copy).then_inc(r_kept, 1)

            def tiles4(i, first=False):
                for m in range(4):
                    n, b2 = 4 * i + m, m % 2
                    exps(n, b2, 0)
                    if not (first and m == 0):
                        keep_p(n - 1, 1 - b2, 3)
                    keep_v(n, b2, 0)
                    exps(n, b2, 1)
                    keep_v(n, b2, 1)
                    keep_p(n, b2, 0)
                    exps(n, b2, 2)
                    exps(n, b2, 3)
                    if not (first and m == 0):
                        keep_r(n - 1)
                    keep_p(n, b2, 1)
                    keep_p(n, b2, 2)

            tiles4(0, first=True)
            with act.Fori(1, NT // 4) as i:
                tiles4(i)
            keep_p(NT - 1, 1, 3)
            keep_r(NT - 1)

        @block.tensor
        def _(pe):
            ident = c("ident")
            pe.wait_ge(consts_in, 16)
            pe.wait_ge(w_in, 16 * 7)
            for half in range(2):
                for o in range(4):
                    ins = pe.transpose(PS[half][:, P * o:P * (o + 1)], W_RAW[:, o, P * half:P * (half + 1)], ident)
                ins.then_inc(turned, 1)
            for e in range(H2):
                for o in range(2):
                    ins = pe.transpose(PS[2][:, D * e + P * o:D * e + P * (o + 1)],
                                       W_RAW[:, 4 + o, P * e:P * (e + 1)], ident)
            ins.then_inc(turned, 1)
            pe.wait_ge(spread_rhs, 2)
            pe.matmul(PS[6][:, 0:2 * NT], c("token_of_seq"), by_tile, start=True, stop=True).then_inc(spread_ps, 1)
            pe.wait_ge(diag_set, 4)
            pe.matmul(PS[7][:, :], c("ones"), DIAG, start=True, stop=True).then_inc(rows_ps, 1)

            def layer0(j, slot):
                pe.wait_ge(w_diag_set, j + 1)
                pe.matmul(PS[slot][:, 0:D], W_DIAG[slot], X[:, bass.ds(D * j, D)], start=True, stop=True).then_inc(l0_done, 1)

            def turn(j, slot):
                pe.wait_ge(x1_set, 2 * j + 2)
                for half in range(2):
                    ins = pe.transpose(PS[2 + slot][:, P * half:P * (half + 1)], X1S[slot][:, P * half:P * (half + 1)], ident)
                ins.then_inc(x1_turned, 1)

            def project(j, slot):
                pe.wait_ge(x1t_set, j + 1)
                for half in range(2):
                    ins = pe.matmul(PS[4 + slot][:, :], X1T[slot][:, P * half:P * (half + 1)], W_QKV[:, half, :],
                                    start=(half == 0), stop=(half == 1))
                ins.then_inc(qkv_done, 1)

            pe.wait_ge(x_in, 32)
            pe.wait_ge(kept_w, 3)
            layer0(0, 0)
            with pe.Fori(0, NG - 1) as i:
                for u in range(2):
                    turn(2 * i + u, u)
                    layer0(2 * i + u + 1, 1 - u)
                    project(2 * i + u, u)
            turn(NT - 2, 0)
            layer0(NT - 1, 1)
            project(NT - 2, 0)
            turn(NT - 1, 1)
            project(NT - 1, 1)
            pe.wait_ge(lhs_set, 1)
            for i in range(2):
                ins = pe.matmul(PS[6][:, NG * i:NG * (i + 1)], LHS[i], c("in_group"), start=True, stop=True)
            ins.then_inc(idx_ps, 1)

            def keys_of(buf, g, b2):
                return buf[:, 512 * g + 256 * b2:512 * g + 256 * b2 + KEYS]

            def turn_v(n, b2, p, ch):
                for g in range(G):
                    ins = pe.transpose(PS[4][0:CH, P * g:P * (g + 1)],
                                       keys_of(VT[p], g, b2)[:, CH * ch:CH * (ch + 1)], ident)
                ins.then_inc(v_turned, 1)

            def turn_p(n, b2, g):
                pe.wait_ge(probs, 8 * n + 2 * g + 2)
                for ch in range(2):
                    for h2 in range(H2):
                        at_ = P * (H2 * ch + h2)
                        ins = pe.transpose(PS[2 + g % 2][0:CH, at_:at_ + P],
                                           PR[b2][:, H2 * g + h2, CH * ch:CH * (ch + 1)], ident)
                ins.then_inc(p_turned, 1)

            def attend(n, b2):
                pe.wait_ge(p_kept, 4 * n + 4)
                pe.wait_ge(v_kept, 2 * n + 2)
                o_ps = PS[5][:, D * b2:D * (b2 + 1)].rearrange("p (e t) -> p e t", e=H2)
                for rg in range(TPS):
                    for ch in range(2):
                        for g in range(G):
                            ins = pe.matmul(
                                o_ps[HD * g:HD * (g + 1), :, T * rg:T * (rg + 1)],
                                VR[b2][0:CH, 512 * ch + P * g + HD * rg:512 * ch + P * g + HD * (rg + 1)],
                                PT[b2][0:CH, 512 * g + 256 * ch:512 * g + 256 * (ch + 1)]
                                .rearrange("p (e t) -> p e t", e=H2)[:, :, T * rg:T * (rg + 1)],
                                start=(ch == 0), stop=(ch == 1), tile_position=(0, HD * g), skip_group_check=True)
                ins.then_inc(summed_o, 1)

            def spread_r(n, b2):
                pe.wait_ge(r_set, n + 1)
                for e in range(H2):
                    ins = pe.matmul(PS[6][:, P * e:P * (e + 1)], R32[b2][:, P * e:P * (e + 1)], ident, start=True, stop=True)
                ins.then_inc(r_spread, 1)

            def project_o(n, b2):
                pe.wait_ge(o_scaled, n + 1)
                for e in range(H2):
                    ins = pe.matmul(PS[7][:, D * b2:D * (b2 + 1)], AT[b2][:, P * e:P * (e + 1)], WO_T[:, D * e:D * (e + 1)],
                                    start=(e == 0), stop=(e == H2 - 1))
                ins.then_inc(y_done, 1)

            def tiles4(i, first=False):
                for m in range(4):
                    n, b2, p = 4 * i + m, m % 2, m // 2
                    if b2 == 0:
                        pe.wait_ge(kt_set, 2 * i + p + 1)
                    before = not (first and m == 0)
                    pe.wait_ge(qd_set, n + 1)
                    for g in range(G):
                        if g >= 2:
                            pe.wait_ge(masked, 8 * n + 2 * (g - 1))
                        elif before:
                            pe.wait_ge(masked, 8 * n + 2 * (g - 1))
                        for h2 in range(H2):
                            ins = pe.matmul(PS[g % 2][:, KEYS * h2:KEYS * (h2 + 1)], QD[b2][:, H2 * g + h2, :],
                                            keys_of(KT[p], g, b2), start=True, stop=True)
                        ins.then_inc(scored, 1)
                        if g == 1:
                            if b2 == 0:
                                pe.wait_ge(vt_set, 2 * i + p + 1)
                            turn_v(n, b2, p, 0)
                            if before:
                                pe.wait_ge(p_kept, 4 * n - 2)
                                turn_p(n - 1, 1 - b2, 3)
                        if g == 2:
                            pe.wait_ge(v_kept, 2 * n + 1)
                            turn_v(n, b2, p, 1)
                            if before:
                                pe.wait_ge(p_kept, 4 * n - 1)
                            turn_p(n, b2, 0)
                    if before:
                        attend(n - 1, 1 - b2)
                        spread_r(n - 1, 1 - b2)
                        pe.wait_ge(p_kept, 4 * n)
                    turn_p(n, b2, 1)
                    pe.wait_ge(p_kept, 4 * n + 1)
                    turn_p(n, b2, 2)
                    if before:
                        project_o(n - 1, 1 - b2)

            tiles4(0, first=True)
            with pe.Fori(1, NT // 4) as i:
                tiles4(i)
            pe.wait_ge(p_kept, 4 * NT - 2)
            turn_p(NT - 1, 1, 3)
            attend(NT - 1, 1)
            spread_r(NT - 1, 1)
            project_o(NT - 1, 1)


def kernel(x, itok_B_1_198, itok_Bx257_0_4111, itok_B_37_3939, L0_cond_weights, L1_cond_Wq, L1_cond_Wk, L1_cond_Wv,
           L1_cond_Wo, L1_cond_q_norm_scale, L1_cond_k_norm_scale, L1_cond_k_blocks, L1_cond_v_blocks):
    import concourse.bacc as bacc
    from concourse.bass_utils import run_bass_kernel_spmd

    nc = bacc.Bacc("TRN2", target_bir_lowering=False, num_devices=1)
    table, at = constants()
    ins = {
        "x": x, "cond": itok_B_1_198, "table": itok_Bx257_0_4111, "kv_lens": itok_B_37_3939, "l0_w": L0_cond_weights,
        "wq": L1_cond_Wq, "wk": L1_cond_Wk, "wv": L1_cond_Wv, "wo": L1_cond_Wo,
        "q_scale": L1_cond_q_norm_scale, "k_scale": L1_cond_k_norm_scale,
        "k_blocks": L1_cond_k_blocks, "v_blocks": L1_cond_v_blocks, "consts": table,
    }
    arrays = {f"in_{n}": np.ascontiguousarray(a) for n, a in ins.items()}
    aps = {n: nc.dram_tensor(f"in_{n}", a.shape, mybir.dt.from_np(a.dtype), kind="ExternalInput").ap()
           for n, a in ((k[3:], v) for k, v in arrays.items())}
    out = nc.dram_tensor("out", (B, T, D), F32, kind="ExternalOutput").ap()
    build(nc, at, out=out, **aps)
    return run_bass_kernel_spmd(nc, [arrays], core_ids=[0]).results[0]["out"]
```

```python
import numpy as np
import concourse.bass as bass
from concourse import mybir
from contextlib import ExitStack

F32 = mybir.dt.float32
I32 = mybir.dt.int32
ALU = mybir.AluOpType
ACT = mybir.ActivationFunctionType
AX = mybir.AxisListType

P = 128
B, T, D = 128, 32, 256
H, G, HD = 8, 4, 32
H2 = H // G
HALF = HD // 2
BLOCK, WINDOW = 16, 128
NBLK = 257
CACHE = 16 * NBLK
CONDS = 200
EPS = 1e-6
THETA = 10000.0
SCALE = 256.0 ** (-0.5)
BW = G * BLOCK * HD
TOK = G * HD

TPS = P // T
NT = B // TPS
NG = NT // 2
SLOTS = 11
PADDED = 16
BACK = WINDOW // BLOCK
WR = 3
KEYS = SLOTS * BLOCK
CH = KEYS // 2
NW = WR * B
SPREAD = (0, 2, 1)
ORDER = (2, 0, 1)
SKIP = 65536.0
BIG = float(2.0 ** 100)
HUGE = 3.0e38
TWO_PI_A, TWO_PI_B = 6.28125, 0.0019350051879882812
TWO_PI_C = float(2 * np.pi - TWO_PI_A - TWO_PI_B)
ROUND = float(1.5 * 2 ** 23)
PI_IN = 3.1415925


def constants():
    p = np.arange(P)
    key_slot, key_off = np.arange(KEYS) // BLOCK, np.arange(KEYS) % BLOCK
    dist = (BLOCK * (key_slot - BACK) + key_off).astype(np.float64)
    row = lambda a: np.tile(np.asarray(a, np.float64).reshape(1, -1), (P, 1))
    parts = {
        "ident": np.eye(P),
        "ones": np.ones((P, P)),
        "same_quadrant": (p[:, None] // T == p[None, :] // T),
        "token_of_seq": (p[:, None] % TPS == p[None, :] // T),
        "seq_of_slot": (p[:, None] % (2 * TPS) == row(np.arange(8))[:1] % 2 * TPS + row(np.arange(8))[:1] // 2),
        "in_group": (p[:, None] // 8 == np.arange(NG)[None, :]),
        "in_tile": (p[:, None] // TPS == np.arange(NT)[None, :]),
        "eye_t": (p[:, None] % T == np.arange(HD)[None, :]),
        "t": (p % T)[:, None],
        "eps": np.full((P, 1), EPS),
        "slot": row(np.arange(SLOTS)),
        "column": row(np.arange(NBLK)),
        "inv_freq": row(1.0 / np.float32(THETA) ** (np.arange(HALF, dtype=np.float32) / np.float32(HALF))),
        "off": row(np.arange(BLOCK)),
        "first_code": row(T * np.arange(B) + BLOCK + 1),
        "dist": row(dist * BIG),
        "neg_dist": row(-dist * BIG),
        "writer": row([B * j + b + 1 for j in SPREAD for b in range(B)]),
    }
    at, n = {}, 0
    for name, a in parts.items():
        at[name] = (n, a.shape[1])
        n += a.shape[1]
    return np.concatenate([a.astype(np.float32) for a in parts.values()], axis=1), at


def build(nc, at, x, cond, table, kv_lens, l0_w, wq, wk, wv, wo, q_scale, k_scale, k_blocks, v_blocks, consts, out):
    with ExitStack() as ctx:
        def sb(name, cols, dt=F32):
            return ctx.enter_context(nc.sbuf_tensor(name, [P, cols], dt))

        def sem(name):
            return ctx.enter_context(nc.semaphore(name))

        l0_rows = nc.dram_tensor("l0_rows", (B, T * HD), F32, kind="Internal").ap()
        new_kv = nc.dram_tensor("new_kv", (B * T, 2 * TOK), F32, kind="Internal").ap()
        upd = [nc.dram_tensor(n, (NW, BW), F32, kind="Internal").ap() for n in ("updated_k", "updated_v")]

        X = sb("x_res", NT * D)
        Q = sb("q_rows", NT * D)
        CST = sb("consts", consts.shape[1])
        WO_T = sb("wo_t", H2 * D)
        WQ_T = sb("wq_t", 2 * D)[:, :]
        RSTD_Q = sb("rstd_q", NT * H)
        ROWS = sb("rows", 512)[:, :]
        small = sb("small", 520)
        ints = sb("ints", 120, I32)
        ARENA = sb("arena", 31744)

        def c(name, a=0, b=None):
            s, n = at[name]
            return CST[:, s + a:s + (n if b is None else b)]

        x3 = X[:, :].rearrange("p (j d) -> p j d", d=D)
        q3 = Q[:, :].rearrange("p (j d) -> p j d", d=D)
        used = [0]

        def cut(n):
            s = used[0]
            used[0] += n
            return small[:, s:s + n]

        kv_f, a_f, r_f = cut(1), cut(1), cut(1)
        slot_no, blk = cut(SLOTS), cut(PADDED)
        by_tile = cut(2 * NT)
        pos, hi, lo = cut(NT), cut(NT), cut(NT)
        qk_gain = cut(4 * HD)
        match, miss = cut(SLOTS), cut(SLOTS)
        ss, sd = cut(HD), cut(HD)
        won, won_whole = cut(WR * BLOCK), cut(WR)
        assert used[0] <= 520
        n_cols = [0]

        def icut(n):
            s = n_cols[0]
            n_cols[0] += n
            return ints[:, s:s + n]

        kv_i, a_i, cond_i = icut(1), icut(1), icut(1)
        base_idx, win_idx = icut(WR), icut(WR * BLOCK)
        idx_cache, idx_upd = icut(NG), icut(NG)

        def region(s, n):
            return ARENA[:, s:s + n]

        BASE = [[region(4096 * j + 2048 * kv, BW) for kv in range(2)] for j in range(WR)]
        W_RAW = region(8192, 1536).rearrange("p (o d) -> p o d", d=D)
        TBL_I = ARENA[:, 9728:9728 + NBLK].bitcast(I32)
        TBL = region(9728 + NBLK, NBLK)
        ANG = [region(10242 + 512 * i, NT * HALF) for i in range(3)]
        R0 = 12288
        MERGE = [region(R0 + 4096 * j, BLOCK * 2 * TOK) for j in range(WR)]
        ROW = region(R0, NT * 2 * TOK).rearrange("p (j c) -> p j c", c=2 * TOK)
        A1 = R0 + 8192
        L0_W = region(A1, NT * HD).rearrange("p (j d) -> p j d", d=HD)
        W_DIAG = [region(A1 + 1024 + P * i, P) for i in range(8)]
        W_DIAG4 = [region(A1 + 1024 + 512 * i, 512).rearrange("p (j s d) -> p j s d", j=4, s=TPS) for i in range(2)]
        W_KV = region(A1 + 2048, 2 * D).rearrange("p (c n) -> p c n", c=2)
        X1S = [region(A1 + 2560 + D * i, D) for i in range(2)]
        X1T = [region(A1 + 3072 + D * i, D) for i in range(2)]
        SQ, TA, TB = (region(24576 + 1024 * i, 1024) for i in range(3))
        DIAG = SQ[:, 0:512]
        JUNK = [region(25600 + 2 * B * i, 2 * B) for i in range(8)]
        TABS = [region(27648 + 1024 * i, NT * HD).rearrange("p (j d) -> p j d", d=HD) for i in range(4)]
        COS_Q, SIN_Q, COS_K, SIN_K = TABS
        SS_K, SD_K = RSTD_Q[:, 0:NT * G], RSTD_Q[:, NT * G:2 * NT * G]
        def spare(at_, n):
            return Q[:, T * HD + at_:T * HD + at_ + n]

        MATCHES = spare(0, SLOTS * NW)
        CAND = spare(0, BLOCK * 2 * B).rearrange("p (o j b) -> p o j b", j=2, b=B)
        COVERS = spare(4224, BLOCK * B).rearrange("p (o b) -> p o b", b=B)
        EQ = spare(4224, WR * NW)
        LHS = [spare(4224 + WR * NW + P * i, P) for i in range(2)]
        CODE = spare(4224 + 2048, WR * B)
        XQS = sb("xq_now", D)[:, :]
        XQT = [sb(f"xq_turned{i}", D)[:, :] for i in range(2)]

        KG = [region(24576, BW), region(28672, BW)]
        VG = [region(26624, BW), region(0, BW)]
        KT = [region(12288, BW), region(2048, BW)]
        VT = [region(14336, BW), region(4096, BW)]
        PR = [region(6144 + H * KEYS * i, H * KEYS).rearrange("p (h k) -> p h k", k=KEYS) for i in range(2)]
        QD = [region(8960 + 1024 * i, 1024).rearrange("p (h n) -> p h n", n=P) for i in range(2)]
        AT = [region(11008 + D * i, D) for i in range(2)]
        R32 = [region(11520 + D * i, D) for i in range(2)]
        RB = region(12032, D)
        PT = [region(16384 + 2048 * i, 2048) for i in range(2)]
        VR = [region(20480 + 1024 * i, 1024) for i in range(2)]
        Y = [region(22528 + D * i, D) for i in range(2)]
        QS = [region(23040 + D * i, D) for i in range(2)]
        MASK = [region(23552 + KEYS * i, KEYS) for i in range(2)]
        LOWER = region(23904, KEYS)
        NMAX = [region(24080 + H * i, H) for i in range(2)]
        SUMS = [region(24096 + H * i, H) for i in range(2)]

        PS = [ctx.enter_context(nc.psum_tensor(f"bank{i}", [P, 512], F32)) for i in range(8)]

        S_BANK = ((0, 1, 2, 0), (1, 2, 0, 1))
        S_AGO = ((2, 2, 5, 3), (3, 3, 3, 3))
        O_PS, R_PS, Y_PS = PS[6][:, 0:D], PS[7][:, 0:D], PS[7][:, D:2 * D]

        consts_in, ints_in, w_in, gain_in, l0_got, l0_kept, l0_in = (sem(n) for n in (
            "consts_in", "ints_in", "w_in", "gain_in", "l0_got", "l0_kept", "l0_in"))
        x_first_in, x_in, cond_in = sem("x_first_in"), sem("x_in"), sem("cond_in")
        dve_step, pool_step, act_step = sem("dve_step"), sem("pool_step"), sem("act_step")
        spread_rhs, spread_ps, diag_set, rows_ps, rows_set = (sem(n) for n in (
            "spread_rhs", "spread_ps", "diag_set", "rows_ps", "rows_set"))
        cand_set, win_set, base_set, lhs_set, idx_ps, idx_set = (sem(n) for n in (
            "cand_set", "win_set", "base_set", "lhs_set", "idx_ps", "idx_set"))
        turned, kept_w, angles, sines, cosines, gains, tables_q, tables_k = (sem(n) for n in (
            "turned", "kept_w", "angles", "sines", "cosines", "gains", "tables_q", "tables_k"))
        l0_w_set, w_diag_set, l0_done, x1s_set, x1_kept, x1_turned, x1t_set, kv_done, kv_kept = (sem(n) for n in (
            "l0_w_set", "w_diag_set", "l0_done", "x1s_set", "x1_kept", "x1_turned", "x1t_set", "kv_done", "kv_kept"))
        k_squared, k_crossed, k_summed, k_added, k_root, k_roped, kv_stored = (sem(n) for n in (
            "k_squared", "k_crossed", "k_summed", "k_added", "k_root", "k_roped", "kv_stored"))
        xq_set, xq_turned, xqt_set, q_done, q_kept = (sem(n) for n in (
            "xq_set", "xq_turned", "xqt_set", "q_done", "q_kept"))
        base_in = [sem(f"base_in{j}") for j in range(WR)]
        won_in = [sem(f"won_in{j}") for j in range(WR)]
        laid_k, laid_v, laid_v2, merged_k, merged_v = (sem(n) for n in (
            "laid_k", "laid_v", "laid_v2", "merged_k", "merged_v"))
        upd_stored = [sem(f"upd_stored{j}") for j in range(WR)]
        q_squared, q_summed, q_root, q_rstd = (sem(n) for n in ("q_squared", "q_summed", "q_root", "q_rstd"))
        cleared = sem("cleared")
        k_in = [sem(f"k_in{i}") for i in range(2)]
        v_in = [sem(f"v_in{i}") for i in range(2)]
        kt_set, vt_set, q_scaled, qd_set, mask_set = (sem(n) for n in (
            "kt_set", "vt_set", "q_scaled", "qd_set", "mask_set"))
        scored, masked, probs, p_turned, p_kept, v_turned, v_kept = (sem(n) for n in (
            "scored", "masked", "probs", "p_turned", "p_kept", "v_turned", "v_kept"))
        inverted, r_set, r_spread, r_kept, summed_o, o_scaled, y_done, y_set = (sem(n) for n in (
            "inverted", "r_set", "r_spread", "r_kept", "summed_o", "o_scaled", "y_done", "y_set"))
        y_sent = [sem(f"y_sent{i}") for i in range(2)]

        KC, KN = 4, NT // 4
        QC, QN = 8, NT // 8

        def table_parts(cos_tab, sin_tab, g0):
            sin, cos = (a.rearrange("p (j f) -> p j f", f=HALF) for a in (ANG[1], ANG[2]))
            return [(tab[:, :, HALF * half:HALF * (half + 1)], trig,
                     qk_gain[:, g0 + g:g0 + g + HALF].unsqueeze(1).to_broadcast([P, NT, HALF]))
                    for tab, half, trig, g in ((cos_tab, 0, cos, 0), (cos_tab, 1, cos, HALF),
                                               (sin_tab, 0, sin, HD + HALF), (sin_tab, 1, sin, 0))]

        def lay(copy, merge, base, kv, done, *more):
            copy(merge.rearrange("p (o c) -> p o c", o=BLOCK)[:, :, TOK * kv:TOK * (kv + 1)]
                 .rearrange("p o (g d) -> p g o d", g=G),
                 base[kv].rearrange("p (g o d) -> p g o d", g=G, o=BLOCK), *more).then_inc(done, 1)

        def lay_back(copy, base, merge, kv, done, *more):
            copy(base[kv].rearrange("p (g o d) -> p g o d", g=G, o=BLOCK),
                 merge.rearrange("p (o c) -> p o c", o=BLOCK)[:, :, TOK * kv:TOK * (kv + 1)]
                 .rearrange("p o (g d) -> p g o d", g=G), *more).then_inc(done, 1)

        block = ctx.enter_context(nc.Block())

        @block.sync
        def _(sp):
            sp.dma_start(kv_i, kv_lens.rearrange("(b o) -> b o", o=1)).then_inc(ints_in, 16)
            sp.dma_start(TBL_I, table).then_inc(ints_in, 16)
            sp.dma_start(CST[:, :], consts).then_inc(consts_in, 16)
            sp.dma_start(W_RAW[:, 0:2, :], wq.rearrange("(o p) d -> p o d", p=P)).then_inc(w_in, 16)
            sp.dma_start(W_RAW[:, 2, :], wk).then_inc(w_in, 16)
            sp.dma_start(W_RAW[:, 3, :], wv).then_inc(w_in, 16)
            sp.wait_ge(l0_got, 16)
            sp.dma_start(l0_rows, Q[:, 0:T * HD]).then_inc(l0_kept, 16)
            sp.dma_start(qk_gain[:, 0:HD], q_scale.rearrange("(o d) -> o d", o=1).to_broadcast([P, HD])).then_inc(gain_in, 16)
            sp.dma_start(qk_gain[:, 2 * HD:3 * HD], k_scale.rearrange("(o d) -> o d", o=1).to_broadcast([P, HD])).then_inc(gain_in, 16)
            for o in range(2):
                for e in range(H2):
                    sp.dma_start(W_RAW[:, 4 + o, P * e:P * (e + 1)].rearrange("p (g d) -> p g d", d=HD),
                                 wo[P * o:P * (o + 1), :].rearrange("p (g e d) -> p e g d", e=H2, d=HD)[:, e]).then_inc(w_in, 16)
            x_tiles = x.rearrange("(j s) c t -> (s c) j t", s=TPS)
            for n in range(4):
                if n == 1:
                    sp.wait_ge(l0_kept, 16)
                    sp.dma_start(L0_W, l0_rows.rearrange("(j s) (c d) -> (s c) j d", s=TPS, d=HD)).then_inc(l0_in, 16)
                sp.dma_start(x3[:, 8 * n:8 * n + 8, :], x_tiles[:, 8 * n:8 * n + 8, :]).then_inc(x_in if n else x_first_in, 16)
            for n in range(KC):
                sp.wait_ge(k_roped, n + 1)
                sp.dma_start(new_kv.rearrange("(j p) c -> p j c", p=P)[:, KN * n:KN * (n + 1), :],
                             ROW[:, KN * n:KN * (n + 1), :]).then_inc(kv_stored, 16)
            for i, j in enumerate(ORDER):
                sp.wait_ge(merged_k, i + 1)
                sp.dma_start(upd[0][P * j:P * (j + 1), :], BASE[j][0]).then_inc(upd_stored[j], 16)
                sp.wait_ge(merged_v, i + 1)
                sp.dma_start(upd[1][P * j:P * (j + 1), :], BASE[j][1]).then_inc(upd_stored[j], 16)
            out_tiles = out.rearrange("(j s) c t -> j (s c) t", s=TPS)
            with sp.Fori(0, NG) as g:
                for b2 in range(2):
                    sp.wait_ge(y_set, 2 * g + b2 + 1)
                    sp.dma_start(out_tiles[bass.ds(2 * g + b2, 1)].rearrange("o p t -> p (o t)"),
                                 Y[b2]).then_inc(y_sent[b2], 16)
            for b2 in range(2):
                sp.wait_ge(y_sent[b2], 16 * NG)

        @block.gpsimd
        def _(pool):
            steps = [0]

            def link(ins):
                steps[0] += 1
                ins.then_inc(pool_step, 1)
                pool.wait_ge(pool_step, steps[0])

            pool.dma_start(cond_i, cond.rearrange("(b o) -> b o", o=1)).then_inc(cond_in, 16)
            pool.wait_ge(cond_in, 16)
            pool.indirect_dma_start(Q[:, 0:T * HD], None, l0_w.rearrange("s c d -> s (c d)"),
                                    bass.IndirectOffsetOnAxis(cond_i, 0), bounds_check=CONDS - 1,
                                    oob_is_err=False).then_inc(l0_got, 16)
            pool.wait_ge(l0_in, 16)
            pool.wait_ge(consts_in, 16)

            def add_eye(n):
                pool.tensor_tensor(L0_W[:, 8 * n:8 * n + 8, :], L0_W[:, 8 * n:8 * n + 8, :],
                                   c("eye_t").unsqueeze(1).to_broadcast([P, 8, HD]), ALU.add).then_inc(l0_w_set, 1)
                pool.wait_ge(l0_w_set, n + 1)

            def w_diag(q):
                if q >= 2:
                    pool.wait_ge(l0_done, 4 * (q - 1))
                wide = [P, 4, TPS, HD]
                pool.tensor_tensor(W_DIAG4[q % 2], L0_W[:, 4 * q:4 * q + 4, :].unsqueeze(2).to_broadcast(wide),
                                   c("same_quadrant").rearrange("p (s d) -> p s d", s=TPS).unsqueeze(1).to_broadcast(wide),
                                   ALU.mult).then_inc(w_diag_set, 1)

            def table_q(n):
                pool.tensor_tensor(*table_parts(COS_Q, SIN_Q, 0)[n], ALU.mult).then_inc(tables_q, 1)

            def key_squares(n):
                k = ROW[:, KN * n:KN * (n + 1), 0:TOK]
                pool.wait_ge(kv_kept, KN * (n + 1))
                if n:
                    pool.wait_ge(k_summed, n)
                pool.tensor_tensor(SQ.rearrange("p (j c) -> p j c", c=TOK), k, k, ALU.mult).then_inc(k_squared, 1)

            def get_base(j):
                for kv, cache in enumerate((k_blocks, v_blocks)):
                    pool.indirect_dma_start(BASE[j][kv], None, cache.rearrange("n g o d -> n (g o d)"),
                                            bass.IndirectOffsetOnAxis(base_idx[:, j:j + 1], 0),
                                            bounds_check=CACHE - 1, oob_is_err=False).then_inc(base_in[j], 16)

            for q in range(8):
                if q % 2 == 0:
                    add_eye(q // 2)
                w_diag(q)
                if q == 1:
                    pool.wait_ge(base_set, 1)
                    get_base(0)
                    get_base(1)
                    pool.wait_ge(cosines, 1)
                    pool.wait_ge(gains, 1)
                if q in (2, 3):
                    table_q(2 * q - 4)
                    table_q(2 * q - 3)
                if q == 4:
                    pool.wait_ge(kept_w, 5)
                    pool.wait_ge(tables_k, 4)
                    pool.wait_ge(tables_q, 4)
                    get_base(2)
                if q == 5:
                    key_squares(0)
            for n in range(1, KC - 1):
                key_squares(n)
            pool.wait_ge(base_in[2], 32)
            pool.wait_ge(kv_done, NT)
            lay(pool.tensor_copy, MERGE[2], BASE[2], 1, laid_v2)
            pool.wait_ge(win_set, 1)
            pool.wait_ge(kv_stored, 16 * KC)
            for i, j in enumerate(ORDER):
                pool.wait_ge(laid_k, i + 1)
                if i:
                    pool.wait_ge(laid_v, i)
                else:
                    pool.wait_ge(laid_v2, 1)
                for o in range(BLOCK):
                    pool.indirect_dma_start(MERGE[j][:, 2 * TOK * o:2 * TOK * (o + 1)], None, new_kv,
                                            bass.IndirectOffsetOnAxis(win_idx[:, BLOCK * j + o:BLOCK * j + o + 1], 0),
                                            bounds_check=B * T - 1, oob_is_err=False).then_inc(won_in[j], 16)

            def gather_cache(g, buf, got, cache):
                pool.indirect_dma_start(buf[g % 2], None, cache.rearrange("n g o d -> n (g o d)"),
                                        bass.IndirectOffsetOnAxis(idx_cache[:, g:g + 1], 0),
                                        bounds_check=CACHE - 1, oob_is_err=False).then_inc(got[g % 2], 16)

            def gather_new(g, buf, got, new):
                pool.wait_ge(got[g % 2], 32 * (g // 2) + 16)
                pool.indirect_dma_start(buf[g % 2], None, new,
                                        bass.IndirectOffsetOnAxis(idx_upd[:, g:g + 1], 0),
                                        bounds_check=NW - 1, oob_is_err=False).then_inc(got[g % 2], 16)

            def gather(g, buf, got, cache, new):
                gather_cache(g, buf, got, cache)
                gather_new(g, buf, got, new)

            keys, values = (KG, k_in, k_blocks, upd[0]), (VG, v_in, v_blocks, upd[1])
            pool.wait_ge(idx_set, 2)
            pool.wait_ge(cleared, 3)
            gather_cache(0, *keys[:3])
            gather_cache(0, *values[:3])
            gather_cache(1, *keys[:3])
            pool.wait_ge(cleared, 4)
            gather_cache(1, *values[:3])
            for j in range(WR):
                pool.wait_ge(upd_stored[j], 32)
            for g in range(2):
                for what in (keys, values):
                    gather_new(g, what[0], what[1], what[3])
            pool.wait_ge(q_rstd, QC)
            for n in range(NT):
                if n >= 2:
                    pool.wait_ge(qd_set, n - 1)
                pool.tensor_tensor(QS[n % 2].rearrange("p (h d) -> p h d", d=HD),
                                   q3[:, n, :].rearrange("p (h d) -> p h d", d=HD),
                                   RSTD_Q[:, H * n:H * (n + 1)].unsqueeze(2).to_broadcast([P, H, HD]),
                                   ALU.mult).then_inc(q_scaled, 1)
                if n // 2 + 2 < NG:
                    if n % 2 == 0:
                        pool.wait_ge(kt_set, n + 2)
                        gather(n // 2 + 2, *keys)
                    else:
                        pool.wait_ge(vt_set, n + 1)
                        gather(n // 2 + 2, *values)

        @block.vector
        def _(dve):
            steps = [0]

            def link(ins):
                steps[0] += 1
                ins.then_inc(dve_step, 1)
                dve.wait_ge(dve_step, steps[0])

            dve.wait_ge(ints_in, 32)
            link(dve.tensor_scalar(a_i, kv_i, 4, None, ALU.arith_shift_right))
            dve.tensor_copy(kv_f, kv_i).then_inc(dve_step, 1)
            dve.tensor_copy(TBL, TBL_I).then_inc(dve_step, 1)
            steps[0] += 2
            link(dve.tensor_copy(a_f, a_i))
            dve.wait_ge(consts_in, 16)
            dve.tensor_scalar(by_tile[:, 0:NT], c("in_tile"), kv_f, None, ALU.mult).then_inc(spread_rhs, 1)
            dve.tensor_scalar(by_tile[:, NT:2 * NT], c("in_tile"), a_f, None, ALU.mult).then_inc(spread_rhs, 1)
            link(dve.scalar_tensor_tensor(r_f, a_f, -float(BLOCK), kv_f, ALU.mult, ALU.add))
            link(dve.tensor_scalar(slot_no, c("slot"), a_f, -float(BACK), ALU.add, ALU.add))
            link(dve.tensor_scalar(slot_no, slot_no, 0.0, float(NBLK - 1), ALU.max, ALU.min))
            link(dve.memset(blk, SKIP))
            for s in range(SLOTS):
                dve.scalar_tensor_tensor(MATCHES[:, NBLK * s:NBLK * (s + 1)], c("column"), slot_no[:, s:s + 1], TBL,
                                         ALU.is_equal, ALU.mult, accum_out=blk[:, s:s + 1]).then_inc(dve_step, 1)
            steps[0] += SLOTS
            dve.wait_ge(dve_step, steps[0])
            for j in range(WR):
                dve.tensor_scalar(DIAG[:, B * j:B * (j + 1)], c("ident"), blk[:, BACK + SPREAD[j]:BACK + SPREAD[j] + 1], None,
                                  ALU.mult).then_inc(diag_set, 1)
            dve.tensor_scalar(DIAG[:, NW:NW + B], c("ident"), r_f, None, ALU.mult).then_inc(diag_set, 1)
            dve.tensor_copy(base_idx, blk[:, BACK:BACK + WR]).then_inc(base_set, 1)
            dve.wait_ge(spread_ps, 1)
            link(dve.tensor_scalar(pos, PS[6][:, 0:NT], c("t"), None, ALU.add))
            link(dve.scalar_tensor_tensor(hi, PS[6][:, NT:2 * NT], -float(BLOCK), pos, ALU.mult, ALU.add))
            link(dve.tensor_scalar(lo, hi, -float(WINDOW - 1), None, ALU.add))
            link(dve.scalar_tensor_tensor(lo, PS[6][:, NT:2 * NT], -float(BLOCK), lo, ALU.mult, ALU.max))
            link(dve.tensor_scalar(hi, hi, BIG, None, ALU.mult))
            link(dve.tensor_scalar(lo, lo, BIG, None, ALU.mult))
            a0, a1, a2 = ANG
            grid = lambda a: a.rearrange("p (j f) -> p j f", f=HALF)
            link(dve.tensor_tensor(grid(a0), pos.unsqueeze(2).to_broadcast([P, NT, HALF]),
                                   c("inv_freq").unsqueeze(1).to_broadcast([P, NT, HALF]), ALU.mult))
            link(dve.tensor_scalar(a1, a0, float(1 / (2 * np.pi)), ROUND, ALU.mult, ALU.add))
            link(dve.tensor_scalar(a1, a1, ROUND, None, ALU.subtract))
            for part in (TWO_PI_A, TWO_PI_B, TWO_PI_C):
                link(dve.scalar_tensor_tensor(a0, a1, -part, a0, ALU.mult, ALU.add))
            dve.tensor_scalar(a0, a0, PI_IN, -PI_IN, ALU.min, ALU.max).then_inc(angles, 1)
            dve.wait_ge(gain_in, 32)
            link(dve.tensor_scalar(qk_gain[:, 0:HD], qk_gain[:, 0:HD], 1.0, -SCALE, ALU.add, ALU.mult))
            link(dve.tensor_scalar(qk_gain[:, HD:2 * HD], qk_gain[:, 0:HD], -1.0, None, ALU.mult))
            link(dve.tensor_scalar(qk_gain[:, 2 * HD:3 * HD], qk_gain[:, 2 * HD:3 * HD], 1.0, None, ALU.add))
            dve.tensor_scalar(qk_gain[:, 3 * HD:4 * HD], qk_gain[:, 2 * HD:3 * HD], -1.0, None, ALU.mult).then_inc(gains, 1)
            dve.wait_ge(sines, 2)
            link(dve.tensor_tensor(a2, a2, a2, ALU.mult))
            dve.tensor_scalar(a2, a2, -2.0, 1.0, ALU.mult, ALU.add).then_inc(cosines, 1)
            dve.wait_ge(cosines, 1)
            for part in table_parts(COS_K, SIN_K, 2 * HD):
                dve.tensor_tensor(*part, ALU.mult).then_inc(tables_k, 1)
            dve.wait_ge(rows_set, 1)
            per_off = [P, BLOCK, B]
            r_row = ROWS[:, NW:NW + B]
            codes = [CODE[:, B * j:B * (j + 1)] for j in range(WR)]
            dve.tensor_tensor(COVERS, c("off").unsqueeze(2).to_broadcast(per_off),
                              r_row.unsqueeze(1).to_broadcast(per_off), ALU.is_ge).then_inc(dve_step, 1)
            steps[0] += 1
            link(dve.tensor_tensor(codes[0], c("first_code"), r_row, ALU.subtract))
            for j in (1, 2):
                dve.tensor_scalar(codes[j], codes[0], float(BLOCK * j), None, ALU.add).then_inc(dve_step, 1)
            steps[0] += 2
            dve.wait_ge(dve_step, steps[0])
            dve.tensor_tensor(CAND[:, :, 0, :], COVERS, codes[0].unsqueeze(1).to_broadcast(per_off), ALU.mult).then_inc(dve_step, 1)
            steps[0] += 1
            link(dve.scalar_tensor_tensor(CAND[:, :, 1, :], COVERS, 0.0, codes[2].unsqueeze(1).to_broadcast(per_off),
                                          ALU.is_equal, ALU.mult))
            for j in range(WR):
                dve.tensor_scalar(EQ[:, NW * j:NW * (j + 1)], ROWS[:, 0:NW], blk[:, BACK + j:BACK + j + 1], None,
                                  ALU.is_equal).then_inc(dve_step, 1)
            steps[0] += WR
            dve.wait_ge(dve_step, steps[0])
            first = steps[0]

            def last_writer(n, same, codes_, to):
                if n >= len(JUNK):
                    dve.wait_ge(dve_step, first + n - len(JUNK) + 1)
                dve.tensor_tensor_reduce(out=JUNK[n % len(JUNK)][:, 0:codes_.shape[-1]], in0=same, in1=codes_, scale=1.0,
                                         scalar=0.0, op0=ALU.mult, op1=ALU.max, accum_out=to).then_inc(dve_step, 1)

            for j in range(WR):
                for o in range(BLOCK):
                    last_writer(BLOCK * j + o, EQ[:, NW * j:NW * j + 2 * B], CAND[:, o, :, :].rearrange("p j b -> p (j b)"),
                                won[:, BLOCK * j + o:BLOCK * j + o + 1])
            for j in range(WR):
                last_writer(WR * BLOCK + j, EQ[:, NW * j + 2 * B:NW * (j + 1)], codes[1], won_whole[:, j:j + 1])
            steps[0] = first + WR * (BLOCK + 1)
            dve.wait_ge(dve_step, steps[0])
            won3 = won.rearrange("p (j o) -> p j o", o=BLOCK)
            link(dve.tensor_tensor(won3, won3, won_whole.unsqueeze(2).to_broadcast([P, WR, BLOCK]), ALU.max))
            nobody = JUNK[0][:, 0:WR * BLOCK]
            link(dve.tensor_scalar(nobody, won, 0.0, SKIP, ALU.is_equal, ALU.mult))
            link(dve.tensor_tensor(won3, won3, c("off").unsqueeze(1).to_broadcast([P, WR, BLOCK]), ALU.add))
            dve.scalar_tensor_tensor(win_idx, won, -float(BLOCK + 1), nobody, ALU.add, ALU.add).then_inc(win_set, 1)
            for s in range(SLOTS):
                dve.scalar_tensor_tensor(MATCHES[:, NW * s:NW * (s + 1)], ROWS[:, 0:NW], blk[:, s:s + 1], c("writer"),
                                         ALU.is_equal, ALU.mult).then_inc(dve_step, 1)
            steps[0] += SLOTS
            dve.wait_ge(dve_step, steps[0])
            link(dve.tensor_reduce(match, MATCHES.rearrange("p (s w) -> p s w", w=NW), AX.X, ALU.max))
            link(dve.tensor_scalar(miss, match, 0.0, SKIP, ALU.is_gt, ALU.mult))
            link(dve.tensor_copy(slot_no, blk[:, 0:SLOTS]))
            link(dve.tensor_tensor(blk[:, 0:SLOTS], blk[:, 0:SLOTS], miss, ALU.add))
            lhs = [a.rearrange("p (s k) -> p s k", k=PADDED) for a in LHS]
            place = c("seq_of_slot").unsqueeze(2).to_broadcast([P, 8, PADDED])
            link(dve.tensor_tensor(lhs[0], blk.unsqueeze(1).to_broadcast([P, 8, PADDED]), place, ALU.mult))
            link(dve.tensor_scalar(miss, match, 0.0, SKIP, ALU.is_equal, ALU.mult))
            link(dve.scalar_tensor_tensor(blk[:, 0:SLOTS], match, -1.0, miss, ALU.add, ALU.add))
            dve.tensor_tensor(lhs[1], blk.unsqueeze(1).to_broadcast([P, 8, PADDED]), place, ALU.mult).then_inc(lhs_set, 1)
            for n in range(KC):
                tiles = slice(KN * n, KN * (n + 1))
                k4 = ROW[:, tiles, 0:TOK].rearrange("p j (g d) -> p j g d", d=HD)
                ta, tb = (a.rearrange("p (j g d) -> p j g d", g=G, d=HD) for a in (TA, TB))
                dve.wait_ge(kv_kept, KN * (n + 1))
                dve.tensor_tensor(ta, k4, COS_K[:, tiles, :].unsqueeze(2).to_broadcast([P, KN, G, HD]),
                                  ALU.mult).then_inc(dve_step, 1)
                for half in range(2):
                    dve.tensor_tensor(tb[:, :, :, HALF * half:HALF * (half + 1)],
                                      k4[:, :, :, HALF * (1 - half):HALF * (2 - half)],
                                      SIN_K[:, tiles, HALF * half:HALF * (half + 1)].unsqueeze(2)
                                      .to_broadcast([P, KN, G, HALF]), ALU.mult).then_inc(dve_step, 1)
                steps[0] += 3
                dve.wait_ge(k_squared, n + 1)
                dve.tensor_reduce(SS_K[:, HD * n:HD * (n + 1)], SQ.rearrange("p (h d) -> p h d", d=HD), AX.X,
                                  ALU.add).then_inc(k_summed, 1)
                dve.wait_ge(dve_step, steps[0])
                link(dve.tensor_tensor(k4, ta, tb, ALU.add))
            for n, (a, b) in enumerate(((0, KC - 1), (KC - 1, KC))):
                dve.wait_ge(k_root, n + 1)
                link(dve.reciprocal(SD_K[:, HD * a:HD * b], SD_K[:, HD * a:HD * b]))
                for m in range(a, b):
                    k4 = ROW[:, KN * m:KN * (m + 1), 0:TOK].rearrange("p j (g d) -> p j g d", d=HD)
                    dve.tensor_tensor(k4, k4, SD_K[:, HD * m:HD * (m + 1)].rearrange("p (j g) -> p j g", g=G)
                                      .unsqueeze(3).to_broadcast([P, KN, G, HD]), ALU.mult).then_inc(k_roped, 1)
            dve.wait_ge(k_roped, KC)
            dve.wait_ge(idx_ps, 1)
            dve.tensor_copy(idx_cache, PS[6][:, 0:NG]).then_inc(idx_set, 1)
            dve.tensor_copy(idx_upd, PS[6][:, NG:2 * NG]).then_inc(idx_set, 1)

            base = steps[0]

            def rotate_q(n):
                tiles = bass.ds(QN * n, QN)
                qt = q3[:, tiles, :].rearrange("p j (h d) -> p j h d", d=HD)
                ta, tb = (a.rearrange("p (j h d) -> p j h d", j=QN, h=H) for a in (TA, TB))
                wide = [P, QN, H, HD]
                dve.wait_ge(q_squared, n + 1)
                dve.tensor_reduce(ss, SQ.rearrange("p (h d) -> p h d", d=HD), AX.X, ALU.add).then_inc(q_summed, 1)
                dve.tensor_tensor(ta, qt, COS_Q[:, tiles, :].unsqueeze(2).to_broadcast(wide), ALU.mult).then_inc(dve_step, 1)
                for half in range(2):
                    dve.tensor_tensor(tb[:, :, :, HALF * half:HALF * (half + 1)],
                                      qt[:, :, :, HALF * (1 - half):HALF * (2 - half)],
                                      SIN_Q[:, tiles, HALF * half:HALF * (half + 1)].unsqueeze(2).to_broadcast([P, QN, H, HALF]),
                                      ALU.mult).then_inc(dve_step, 1)
                dve.wait_ge(dve_step, base + 4 * n + 3)
                dve.tensor_tensor(qt, ta, tb, ALU.add).then_inc(dve_step, 1)
                dve.wait_ge(q_root, n + 1)
                dve.reciprocal(RSTD_Q[:, bass.ds(QN * H * n, QN * H)], sd).then_inc(q_rstd, 1)
                dve.wait_ge(dve_step, base + 4 * n + 4)

            dve.wait_ge(tables_q, 4)
            dve.wait_ge(kv_stored, 16 * KC)
            for j in ORDER[1:]:
                dve.wait_ge(base_in[j], 32)
                lay(dve.tensor_copy, MERGE[j], BASE[j], 1, laid_v)
            with dve.Fori(0, QC) as n:
                rotate_q(n)
            steps[0] = base + 4 * QC
            for i, buf in enumerate((KG[0], VG[0], KG[1])):
                dve.memset(buf, 0.0).then_inc(cleared, 1)
            for j in ORDER:
                dve.wait_ge(won_in[j], 16 * BLOCK)
                lay_back(dve.tensor_copy, BASE[j], MERGE[j], 1, merged_v)
            dve.wait_ge(upd_stored[ORDER[1]], 32)
            dve.memset(VG[1], 0.0).then_inc(cleared, 1)

            dve.wait_ge(upd_stored[ORDER[0]], 32)
            for b2 in range(2):
                link(dve.memset(QD[b2], 0.0))

            def turn(buf, turned, got, done, g, p, half):
                dve.wait_ge(got[p], 16 * (g - p) + 32)
                cols = slice(BW // 2 * half, BW // 2 * (half + 1))
                dve.transpose(turned[p][:, cols].rearrange("p (g k o) -> p g o k", g=G // 2, o=BLOCK),
                              buf[p][:, cols].rearrange("p (g o d) -> p g o d", g=G // 2, d=HD)).then_inc(done, 1)

            unit = dve.alloc_register("units_scored")
            dve.reg_mov(unit, 0)

            def spread_q(n, b2):
                dve.wait_ge(q_scaled, n + 1)
                for rg in range(TPS):
                    ins = dve.transpose(QD[b2][T * rg:T * (rg + 1), :, T * rg:T * (rg + 1)],
                                        QS[b2][T * rg:T * (rg + 1), :].rearrange("p (h d) -> p h d", d=HD))
                ins.then_inc(qd_set, 1)

            def mask_lower(n):
                dve.tensor_scalar(LOWER, c("neg_dist"), lo[:, bass.ds(n, 1)], 0.0, ALU.add, ALU.max).then_inc(mask_set, 1)

            def mask(n, b2):
                dve.wait_ge(mask_set, 2 * n + 1)
                dve.scalar_tensor_tensor(MASK[b2], c("dist"), hi[:, bass.ds(n, 1)], LOWER, ALU.subtract, ALU.max).then_inc(mask_set, 1)

            def lower(n, b2, g):
                dve.wait_ge(mask_set, 2 * n + 2)
                dve.reg_add(unit, unit, 1)
                dve.wait_ge(cleared, 4)
                dve.wait_ge(scored, unit)
                for h2 in range(H2):
                    h = H2 * g + h2
                    dve.tensor_tensor_reduce(out=PR[b2][:, h, :], in0=PS[S_BANK[b2][g]][:, KEYS * h2:KEYS * (h2 + 1)],
                                             in1=MASK[b2], scale=1.0, scalar=HUGE, op0=ALU.add, op1=ALU.min,
                                             accum_out=NMAX[b2][:, h:h + 1]).then_inc(masked, 1)

            def invert(n, b2):
                dve.wait_ge(probs, 8 * n + 8)
                dve.reciprocal(SUMS[b2], SUMS[b2]).then_inc(inverted, 1)

            def repeat_r(n, b2):
                dve.wait_ge(inverted, n + 1)
                dve.tensor_copy(R32[b2].rearrange("p (e g d) -> p e g d", e=H2, g=G),
                                SUMS[b2].rearrange("p (g e) -> p e g", e=H2).unsqueeze(3)
                                .to_broadcast([P, H2, G, HD])).then_inc(r_set, 1)

            def scale_o(n, b2):
                dve.wait_ge(summed_o, n + 1)
                dve.wait_ge(r_kept, n + 1)
                dve.tensor_tensor(AT[b2], O_PS, RB, ALU.mult).then_inc(o_scaled, 1)

            def add_res(n, b2, sent):
                dve.wait_ge(y_done, n + 1)
                if sent is not None:
                    dve.wait_ge(y_sent[b2], sent)
                dve.tensor_tensor(Y[b2], Y_PS, X[:, bass.ds(D * n, D)], ALU.add).then_inc(y_set, 1)

            def stage(n, m, i):
                b2, p, loop = m % 2, m // 2 % 2, not isinstance(n, int)
                new, prev, old = loop or n < NT, loop or 1 <= n <= NT, loop or 2 <= n < NT + 2
                g = 2 * i + p
                more = loop or (g + 1 < NG if new else False)
                if new:
                    lower(n, b2, 0)
                if loop or n >= 3:
                    sent = 16 * (g - 2 if b2 == 0 else g - 1)
                    add_res(n - 3, 1 - b2, sent if loop or n >= 5 else None)
                if loop or n + 1 < NT:
                    mask_lower(n + 1)
                    spread_q(n + 1, 1 - b2)
                if new:
                    lower(n, b2, 1)
                if prev:
                    invert(n - 1, 1 - b2)
                if loop or n + 1 < NT:
                    mask(n + 1, 1 - b2)
                if prev:
                    repeat_r(n - 1, 1 - b2)
                turn_args = ((KG, KT, k_in, kt_set), (VG, VT, v_in, vt_set))[b2]
                if more:
                    turn(*turn_args, g + 1, 1 - p, 0)
                if new:
                    lower(n, b2, 2)
                if old:
                    scale_o(n - 2, b2)
                if new:
                    lower(n, b2, 3)
                if more:
                    turn(*turn_args, g + 1, 1 - p, 1)

            dve.wait_ge(merged_k, 1)
            mask_lower(0)
            mask(0, 0)
            spread_q(0, 0)
            for half in range(2):
                turn(KG, KT, k_in, kt_set, 0, 0, half)
            for half in range(2):
                turn(VG, VT, v_in, vt_set, 0, 0, half)
            for n in range(4):
                stage(n, n, 0)
            with dve.Fori(1, NT // 4 - 1) as i:
                for m in range(4):
                    stage(4 * i + m, m, i)
            for n in range(NT - 4, NT + 3):
                stage(n, n % 4, n // 4)

        @block.scalar
        def _(act):
            for half in range(2):
                act.wait_ge(turned, half + 1)
                act.activation(WQ_T[:, D * half:D * (half + 1)], PS[half][:, 0:D], ACT.Copy).then_inc(kept_w, 1)
                act.activation(W_KV[:, half, :], PS[half][:, D:2 * D], ACT.Copy).then_inc(kept_w, 1)
            act.wait_ge(turned, 3)
            act.activation(WO_T[:, :], PS[2][:, :], ACT.Copy).then_inc(kept_w, 1)
            act.wait_ge(rows_ps, 1)
            act.activation(ROWS, PS[7][:, :], ACT.Copy).then_inc(rows_set, 1)
            act.wait_ge(angles, 1)
            act.activation(ANG[1], ANG[0], ACT.Sin).then_inc(sines, 1)
            act.activation(ANG[2], ANG[0], ACT.Sin, scale=0.5).then_inc(sines, 1)

            def stage_x1(j, slot):
                act.wait_ge(l0_done, j + 1)
                act.activation(X1S[slot], PS[slot][:, 0:D], ACT.Copy).then_inc(x1s_set, 1)

            def keep_x1(j, slot):
                act.activation(X[:, bass.ds(D * j, D)], PS[slot][:, 0:D], ACT.Copy).then_inc(x1_kept, 1)

            def turned_x1(j, slot):
                act.wait_ge(x1_turned, j + 1)
                act.activation(X1T[slot], PS[2 + slot][:, 0:D], ACT.Copy).then_inc(x1t_set, 1)

            def keep_kv(j, slot):
                act.wait_ge(kv_done, j + 1)
                act.activation(ROW[:, bass.ds(j, 1), :].rearrange("p o c -> p (o c)"), PS[4 + slot][:, 0:D],
                               ACT.Copy).then_inc(kv_kept, 1)

            def tiles8(k):
                for u in range(8):
                    j, slot = 8 * k + u, u % 2
                    static = isinstance(k, int)
                    turned_x1(j, slot)
                    if not static or j + 1 < NT:
                        stage_x1(j + 1, 1 - slot)
                        keep_x1(j + 1, 1 - slot)
                    if not static or j:
                        keep_kv(j - 1, 1 - slot)

            stage_x1(0, 0)
            keep_x1(0, 0)
            tiles8(0)
            with act.Fori(1, NT // 8 - 1) as k:
                tiles8(k)
            tiles8(NT // 8 - 1)
            keep_kv(NT - 1, 1)

            act.wait_ge(k_summed, KC - 1)
            act.activation(SD_K[:, 0:HD * (KC - 1)], SS_K[:, 0:HD * (KC - 1)], ACT.Sqrt, bias=c("eps"),
                           scale=1.0 / HD).then_inc(k_root, 1)
            act.wait_ge(kv_kept, NT)
            act.activation(SQ.rearrange("p (j c) -> p j c", c=TOK), ROW[:, KN * (KC - 1):NT, 0:TOK],
                           ACT.Square).then_inc(k_squared, 1)
            act.wait_ge(base_in[2], 32)
            act.wait_ge(kv_done, NT)
            lay(act.activation, MERGE[2], BASE[2], 0, laid_k, ACT.Copy)
            act.wait_ge(k_summed, KC)
            act.activation(SD_K[:, HD * (KC - 1):], SS_K[:, HD * (KC - 1):], ACT.Sqrt, bias=c("eps"),
                           scale=1.0 / HD).then_inc(k_root, 1)

            def stage_xq(j):
                act.activation(XQS, X[:, bass.ds(D * j, D)], ACT.Copy).then_inc(xq_set, 1)

            def turned_xq(j, slot):
                act.wait_ge(xq_turned, j + 1)
                act.activation(XQT[slot], PS[2 + slot][:, 0:D], ACT.Copy).then_inc(xqt_set, 1)

            def keep_q(j, slot):
                act.wait_ge(q_done, j + 1)
                act.activation(Q[:, bass.ds(D * j, D)], PS[4 + slot][:, 0:D], ACT.Copy).then_inc(q_kept, 1)

            def root_q(n):
                act.wait_ge(q_summed, n + 1)
                act.activation(sd, ss, ACT.Sqrt, bias=c("eps"), scale=1.0 / HD).then_inc(q_root, 1)

            def chunk_q(n):
                static = isinstance(n, int)
                for u in range(QN):
                    j, slot = QN * n + u, u % 2
                    turned_xq(j, slot)
                    if not static or j + 1 < NT:
                        stage_xq(j + 1)
                    if not static or j:
                        keep_q(j - 1, 1 - slot)
                    if u == 0 and (not static or n):
                        square_q(n - 1)

            def square_q(n):
                if not isinstance(n, int) or n:
                    root_q(n - 1)
                act.wait_ge(q_kept, QN * n + QN)
                act.activation(SQ, Q[:, bass.ds(QN * D * n, QN * D)], ACT.Square).then_inc(q_squared, 1)

            act.wait_ge(x1_kept, NT)
            act.wait_ge(idx_ps, 1)
            stage_xq(0)
            chunk_q(0)
            act.wait_ge(kv_stored, 16 * KC)
            for j in ORDER[1:]:
                act.wait_ge(base_in[j], 32)
                lay(act.activation, MERGE[j], BASE[j], 0, laid_k, ACT.Copy)
            chunk_q(1)
            with act.Fori(2, QC - 1) as n:
                chunk_q(n)
            chunk_q(QC - 1)
            keep_q(NT - 1, 1)
            square_q(QC - 1)
            root_q(QC - 1)
            for j in ORDER:
                act.wait_ge(won_in[j], 16 * BLOCK)
                lay_back(act.activation, BASE[j], MERGE[j], 0, merged_k, ACT.Copy)

            def exps(n, b2, g):
                for h2 in range(H2):
                    h = H2 * g + h2
                    act.wait_ge(masked, 8 * n + h + 1)
                    act.activation(PR[b2][:, h, :], PR[b2][:, h, :], ACT.Exp, bias=NMAX[b2][:, h:h + 1], scale=-1.0,
                                   accum_out=SUMS[b2][:, h:h + 1]).then_inc(probs, 1)

            def keep_p(n, b2, g):
                act.wait_ge(p_turned, 4 * n + g + 1)
                act.activation(PT[b2][0:CH, 512 * g:512 * (g + 1)], PS[3 + g % 2][0:CH, :], ACT.Copy).then_inc(p_kept, 1)

            def keep_v(n, b2, ch):
                act.wait_ge(v_turned, 2 * n + ch + 1)
                act.activation(VR[b2][0:CH, 512 * ch:512 * (ch + 1)], PS[5][0:CH, :], ACT.Copy).then_inc(v_kept, 1)

            def keep_r(n):
                act.wait_ge(r_spread, n + 1)
                act.activation(RB, R_PS, ACT.Copy).then_inc(r_kept, 1)

            def stage(n, m):
                b2, loop = m % 2, not isinstance(n, int)
                new, prev, old = loop or n < NT, loop or 1 <= n <= NT, loop or 2 <= n < NT + 2
                for g in range(G):
                    if new and g < 3:
                        exps(n, b2, g)
                    if old and g == 1:
                        keep_r(n - 2)
                    if prev and g in (1, 2):
                        keep_v(n - 1, 1 - b2, g - 1)
                    if prev:
                        keep_p(n - 1, 1 - b2, g)
                if new:
                    exps(n, b2, 3)

            for n in range(4):
                stage(n, n)
            with act.Fori(1, NT // 4) as i:
                for m in range(4):
                    stage(4 * i + m, m)
            for n in range(NT, NT + 2):
                stage(n, n % 4)

        @block.tensor
        def _(pe):
            ident = c("ident")
            pe.wait_ge(consts_in, 16)
            pe.wait_ge(w_in, 16 * 7)
            for half in range(2):
                for o in range(4):
                    ins = pe.transpose(PS[half][:, P * o:P * (o + 1)], W_RAW[:, o, P * half:P * (half + 1)], ident)
                ins.then_inc(turned, 1)
            for e in range(H2):
                for o in range(2):
                    ins = pe.transpose(PS[2][:, D * e + P * o:D * e + P * (o + 1)],
                                       W_RAW[:, 4 + o, P * e:P * (e + 1)], ident)
            ins.then_inc(turned, 1)
            pe.wait_ge(spread_rhs, 2)
            pe.matmul(PS[6][:, 0:2 * NT], c("token_of_seq"), by_tile, start=True, stop=True).then_inc(spread_ps, 1)
            pe.wait_ge(diag_set, 4)
            pe.matmul(PS[7][:, :], c("ones"), DIAG, start=True, stop=True).then_inc(rows_ps, 1)

            def layer0(k, u):
                if isinstance(k, int) and 8 * k + u == 8:
                    pe.wait_ge(x_in, 48)
                if u % 4 == 0:
                    pe.wait_ge(w_diag_set, 2 * k + u // 4 + 1)
                pe.matmul(PS[u % 2][:, 0:D], W_DIAG[u % 8], X[:, bass.ds(D * (8 * k + u), D)], start=True, stop=True).then_inc(l0_done, 1)

            def project_kv(slot):
                for half in range(2):
                    ins = pe.matmul(PS[4 + slot][:, 0:D], X1T[slot][:, P * half:P * (half + 1)], W_KV[:, half, :],
                                    start=(half == 0), stop=(half == 1))
                ins.then_inc(kv_done, 1)

            def tiles8(k):
                for u in range(8):
                    j, slot = 8 * k + u, u % 2
                    pe.wait_ge(x1s_set, j + 1)
                    for half in range(2):
                        ins = pe.transpose(PS[2 + slot][:, P * half:P * (half + 1)], X1S[slot][:, P * half:P * (half + 1)], ident)
                    ins.then_inc(x1_turned, 1)
                    if not isinstance(k, int) or j + 1 < NT:
                        layer0(k, u + 1)
                    if not isinstance(k, int) or j:
                        project_kv(1 - slot)

            pe.wait_ge(kept_w, 5)
            pe.wait_ge(x_first_in, 16)
            layer0(0, 0)
            tiles8(0)
            with pe.Fori(1, NT // 8 - 1) as k:
                tiles8(k)
            tiles8(NT // 8 - 1)
            pe.wait_ge(x1t_set, NT)
            project_kv(1)
            pe.wait_ge(lhs_set, 1)
            for i in range(2):
                ins = pe.matmul(PS[6][:, NG * i:NG * (i + 1)], LHS[i], c("in_group"), start=True, stop=True)
            ins.then_inc(idx_ps, 1)

            def turn_xq(j, slot):
                pe.wait_ge(xq_set, j + 1)
                for half in range(2):
                    ins = pe.transpose(PS[2 + slot][:, P * half:P * (half + 1)], XQS[:, P * half:P * (half + 1)], ident)
                ins.then_inc(xq_turned, 1)

            def project_q(slot):
                for half in range(2):
                    ins = pe.matmul(PS[4 + slot][:, 0:D], XQT[slot][:, P * half:P * (half + 1)],
                                    WQ_T[:, D * half:D * (half + 1)], start=(half == 0), stop=(half == 1))
                ins.then_inc(q_done, 1)

            turn_xq(0, 0)
            turn_xq(1, 1)
            project_q(0)
            with pe.Fori(1, NT // 2) as i:
                for u in range(2):
                    turn_xq(2 * i + u, u)
                    project_q(1 - u)
            pe.wait_ge(xqt_set, NT)
            project_q(1)

            def keys_of(buf, g, b2):
                return buf[:, 512 * g + 256 * b2:512 * g + 256 * b2 + KEYS]

            def score(n, b2, p, g):
                ago = S_AGO[b2][g]
                if not isinstance(n, int) or 4 * n + g >= ago:
                    pe.wait_ge(masked, 8 * n + 2 * (g - ago + 1))
                for h2 in range(H2):
                    ins = pe.matmul(PS[S_BANK[b2][g]][:, KEYS * h2:KEYS * (h2 + 1)], QD[b2][:, H2 * g + h2, :],
                                    keys_of(KT[p], g, b2), start=True, stop=True)
                ins.then_inc(scored, 1)

            def turn_v(n, b2, p, ch):
                if not isinstance(n, int) or 2 * n + ch >= 1:
                    pe.wait_ge(v_kept, 2 * n + ch)
                for g in range(G):
                    ins = pe.transpose(PS[5][0:CH, P * g:P * (g + 1)],
                                       keys_of(VT[p], g, b2)[:, CH * ch:CH * (ch + 1)], ident)
                ins.then_inc(v_turned, 1)

            def turn_p(n, b2, g):
                if not isinstance(n, int) or 4 * n + g >= 2:
                    pe.wait_ge(p_kept, 4 * n + g - 1)
                pe.wait_ge(probs, 8 * n + 2 * g + 2)
                for ch in range(2):
                    for h2 in range(H2):
                        at_ = P * (H2 * ch + h2)
                        ins = pe.transpose(PS[3 + g % 2][0:CH, at_:at_ + P],
                                           PR[b2][:, H2 * g + h2, CH * ch:CH * (ch + 1)], ident)
                ins.then_inc(p_turned, 1)

            def attend(n, b2):
                if not isinstance(n, int) or n >= 1:
                    pe.wait_ge(o_scaled, n)
                pe.wait_ge(p_kept, 4 * n + 4)
                pe.wait_ge(v_kept, 2 * n + 2)
                o_ps = O_PS.rearrange("p (e t) -> p e t", e=H2)
                for rg in range(TPS):
                    for ch in range(2):
                        for g in range(G):
                            ins = pe.matmul(
                                o_ps[HD * g:HD * (g + 1), :, T * rg:T * (rg + 1)],
                                VR[b2][0:CH, 512 * ch + P * g + HD * rg:512 * ch + P * g + HD * (rg + 1)],
                                PT[b2][0:CH, 512 * g + 256 * ch:512 * g + 256 * (ch + 1)]
                                .rearrange("p (e t) -> p e t", e=H2)[:, :, T * rg:T * (rg + 1)],
                                start=(ch == 0), stop=(ch == 1), tile_position=(0, HD * g), skip_group_check=True)
                ins.then_inc(summed_o, 1)

            def spread_r(n, b2):
                pe.wait_ge(r_set, n + 1)
                if not isinstance(n, int) or n >= 1:
                    pe.wait_ge(y_set, n)
                for e in range(H2):
                    ins = pe.matmul(R_PS[:, P * e:P * (e + 1)], R32[b2][:, P * e:P * (e + 1)], ident, start=True, stop=True)
                ins.then_inc(r_spread, 1)

            def project_o(n, b2):
                pe.wait_ge(o_scaled, n + 1)
                for e in range(H2):
                    ins = pe.matmul(Y_PS, AT[b2][:, P * e:P * (e + 1)], WO_T[:, D * e:D * (e + 1)],
                                    start=(e == 0), stop=(e == H2 - 1))
                ins.then_inc(y_done, 1)

            def stage(n, m):
                b2, p, p_prev = m % 2, m // 2 % 2, (m - 1) // 2 % 2
                loop = not isinstance(n, int)
                new, prev, old = loop or n < NT, loop or 1 <= n <= NT, loop or 2 <= n < NT + 2
                if new:
                    if b2 == 0:
                        pe.wait_ge(kt_set, n + 2)
                    pe.wait_ge(qd_set, n + 1)
                    score(n, b2, p, 0)
                for g in range(G):
                    if old and g == 1:
                        attend(n - 2, b2)
                        spread_r(n - 2, b2)
                    if prev and g in (1, 2):
                        if b2 == 1 and g == 1:
                            pe.wait_ge(vt_set, n + 1)
                        turn_v(n - 1, 1 - b2, p_prev, g - 1)
                    if prev:
                        turn_p(n - 1, 1 - b2, g)
                    if new and g + 1 < G:
                        score(n, b2, p, g + 1)
                if old:
                    project_o(n - 2, b2)

            for n in range(4):
                stage(n, n)
            with pe.Fori(1, NT // 4) as i:
                for m in range(4):
                    stage(4 * i + m, m)
            for n in range(NT, NT + 2):
                stage(n, n % 4)


def kernel(x, itok_B_1_198, itok_Bx257_0_4111, itok_B_37_3939, L0_cond_weights, L1_cond_Wq, L1_cond_Wk, L1_cond_Wv,
           L1_cond_Wo, L1_cond_q_norm_scale, L1_cond_k_norm_scale, L1_cond_k_blocks, L1_cond_v_blocks):
    import concourse.bacc as bacc
    from concourse.bass_utils import run_bass_kernel_spmd

    nc = bacc.Bacc("TRN2", target_bir_lowering=False, num_devices=1)
    table, at = constants()
    ins = {
        "x": x, "cond": itok_B_1_198, "table": itok_Bx257_0_4111, "kv_lens": itok_B_37_3939, "l0_w": L0_cond_weights,
        "wq": L1_cond_Wq, "wk": L1_cond_Wk, "wv": L1_cond_Wv, "wo": L1_cond_Wo,
        "q_scale": L1_cond_q_norm_scale, "k_scale": L1_cond_k_norm_scale,
        "k_blocks": L1_cond_k_blocks, "v_blocks": L1_cond_v_blocks, "consts": table,
    }
    arrays = {f"in_{n}": np.ascontiguousarray(a) for n, a in ins.items()}
    aps = {n: nc.dram_tensor(f"in_{n}", a.shape, mybir.dt.from_np(a.dtype), kind="ExternalInput").ap()
           for n, a in ((k[3:], v) for k, v in arrays.items())}
    out = nc.dram_tensor("out", (B, T, D), F32, kind="ExternalOutput").ap()
    build(nc, at, out=out, **aps)
    return run_bass_kernel_spmd(nc, [arrays], core_ids=[0]).results[0]["out"]
```

```python
import numpy as np
import concourse.bass as bass
from concourse import mybir
from contextlib import ExitStack

F32 = mybir.dt.float32
I32 = mybir.dt.int32
ALU = mybir.AluOpType
ACT = mybir.ActivationFunctionType
AX = mybir.AxisListType

P = 128
B, T, D = 128, 32, 256
H, G, HD = 8, 4, 32
H2 = H // G
HALF = HD // 2
BLOCK, WINDOW = 16, 128
NBLK = 257
CACHE = 16 * NBLK
CONDS = 200
EPS = 1e-6
THETA = 10000.0
SCALE = 256.0 ** (-0.5)
BW = G * BLOCK * HD
TOK = G * HD

TPS = P // T
NT = B // TPS
NG = NT // 2
SLOTS = 11
PADDED = 16
BACK = WINDOW // BLOCK
WR = 3
KEYS = SLOTS * BLOCK
CH = KEYS // 2
NW = WR * B
SPREAD = (0, 2, 1)
ORDER = (2, 0, 1)
SKIP = 65536.0
BIG = float(2.0 ** 100)
HUGE = 3.0e38
TWO_PI_A, TWO_PI_B = 6.28125, 0.0019350051879882812
TWO_PI_C = float(2 * np.pi - TWO_PI_A - TWO_PI_B)
ROUND = float(1.5 * 2 ** 23)
PI_IN = 3.1415925


def constants():
    p = np.arange(P)
    key_slot, key_off = np.arange(KEYS) // BLOCK, np.arange(KEYS) % BLOCK
    dist = (BLOCK * (key_slot - BACK) + key_off).astype(np.float64)
    row = lambda a: np.tile(np.asarray(a, np.float64).reshape(1, -1), (P, 1))
    parts = {
        "ident": np.eye(P),
        "ones": np.ones((P, P)),
        "same_quadrant": (p[:, None] // T == p[None, :] // T),
        "token_of_seq": (p[:, None] % TPS == p[None, :] // T),
        "seq_of_slot": (p[:, None] % (2 * TPS) == row(np.arange(8))[:1] % 2 * TPS + row(np.arange(8))[:1] // 2),
        "in_group": (p[:, None] // 8 == np.arange(NG)[None, :]),
        "in_tile": (p[:, None] // TPS == np.arange(NT)[None, :]),
        "eye_t": (p[:, None] % T == np.arange(HD)[None, :]),
        "t": (p % T)[:, None],
        "eps": np.full((P, 1), EPS),
        "slot": row(np.arange(SLOTS)),
        "column": row(np.arange(NBLK)),
        "inv_freq": row(1.0 / np.float32(THETA) ** (np.arange(HALF, dtype=np.float32) / np.float32(HALF))),
        "off": row(np.arange(BLOCK)),
        "first_code": row(T * np.arange(B) + BLOCK + 1),
        "dist": row(dist * BIG),
        "neg_dist": row(-dist * BIG),
        "writer": row([B * j + b + 1 for j in SPREAD for b in range(B)]),
    }
    at, n = {}, 0
    for name, a in parts.items():
        at[name] = (n, a.shape[1])
        n += a.shape[1]
    return np.concatenate([a.astype(np.float32) for a in parts.values()], axis=1), at


def build(nc, at, x, cond, table, kv_lens, l0_w, wq, wk, wv, wo, q_scale, k_scale, k_blocks, v_blocks, consts, out):
    with ExitStack() as ctx:
        def sb(name, cols, dt=F32):
            return ctx.enter_context(nc.sbuf_tensor(name, [P, cols], dt))

        def sem(name):
            return ctx.enter_context(nc.semaphore(name))

        l0_rows = nc.dram_tensor("l0_rows", (B, T * HD), F32, kind="Internal").ap()
        new_kv = nc.dram_tensor("new_kv", (B * T, 2 * TOK), F32, kind="Internal").ap()
        upd = [nc.dram_tensor(n, (NW, BW), F32, kind="Internal").ap() for n in ("updated_k", "updated_v")]

        X = sb("x_res", NT * D)
        Q = sb("q_rows", NT * D)
        CST = sb("consts", consts.shape[1])
        WO_T = sb("wo_t", H2 * D)
        WQ_T = sb("wq_t", 2 * D)[:, :]
        RSTD_Q = sb("rstd_q", NT * H)
        ROWS = sb("rows", NW + B)[:, :]
        small = sb("small", 520)
        ints = sb("ints", 120, I32)
        ARENA = sb("arena", 31744)

        def c(name, a=0, b=None):
            s, n = at[name]
            return CST[:, s + a:s + (n if b is None else b)]

        x3 = X[:, :].rearrange("p (j d) -> p j d", d=D)
        q3 = Q[:, :].rearrange("p (j d) -> p j d", d=D)
        used = [0]

        def cut(n):
            s = used[0]
            used[0] += n
            return small[:, s:s + n]

        kv_f, a_f, r_f = cut(1), cut(1), cut(1)
        slot_no, blk = cut(SLOTS), cut(PADDED)
        by_tile = cut(2 * NT)
        pos, hi, lo = cut(NT), cut(NT), cut(NT)
        qk_gain = cut(4 * HD)
        match, miss = cut(SLOTS), cut(SLOTS)
        ss, sd = cut(HD), cut(HD)
        won, won_whole = cut(WR * BLOCK), cut(WR)
        assert used[0] <= 520
        n_cols = [0]

        def icut(n):
            s = n_cols[0]
            n_cols[0] += n
            return ints[:, s:s + n]

        kv_i, a_i, cond_i = icut(1), icut(1), icut(1)
        base_idx, win_idx = icut(WR), icut(WR * BLOCK)
        idx_cache, idx_upd = icut(NG), icut(NG)

        def region(s, n):
            return ARENA[:, s:s + n]

        BASE = [[region(4096 * j + 2048 * kv, BW) for kv in range(2)] for j in range(WR)]
        W_RAW = region(8192, 1536).rearrange("p (o d) -> p o d", d=D)
        TBL_I = ARENA[:, 9728:9728 + NBLK].bitcast(I32)
        TBL = region(9728 + NBLK, NBLK)
        ANG = [region(10242 + 512 * i, NT * HALF) for i in range(3)]
        R0 = 12288
        MERGE = [region(R0 + 4096 * j, BLOCK * 2 * TOK) for j in range(WR)]
        ROW = region(R0, NT * 2 * TOK).rearrange("p (j c) -> p j c", c=2 * TOK)
        A1 = R0 + 8192
        L0_W = region(A1, NT * HD).rearrange("p (j d) -> p j d", d=HD)
        W_DIAG = [region(A1 + 1024 + P * i, P) for i in range(8)]
        W_DIAG4 = [region(A1 + 1024 + 512 * i, 512).rearrange("p (j s d) -> p j s d", j=4, s=TPS) for i in range(2)]
        W_KV = region(A1 + 2048, 2 * D).rearrange("p (c n) -> p c n", c=2)
        X1S = [region(A1 + 2560 + D * i, D) for i in range(2)]
        X1T = [region(A1 + 3072 + D * i, D) for i in range(2)]
        SQ, TA, TB = (region(24576 + 1024 * i, 1024) for i in range(3))
        DIAG = SQ[:, 0:512]
        JUNK = [region(25600 + 2 * B * i, 2 * B) for i in range(8)]
        TABS = [region(27648 + 1024 * i, NT * HD).rearrange("p (j d) -> p j d", d=HD) for i in range(4)]
        COS_Q, SIN_Q, COS_K, SIN_K = TABS
        SS_K, SD_K = RSTD_Q[:, 0:NT * G], RSTD_Q[:, NT * G:2 * NT * G]
        def spare(at_, n):
            return Q[:, T * HD + at_:T * HD + at_ + n]

        MATCHES = spare(0, SLOTS * NW)
        CAND = spare(0, BLOCK * 2 * B).rearrange("p (o j b) -> p o j b", j=2, b=B)
        COVERS = spare(4224, BLOCK * B).rearrange("p (o b) -> p o b", b=B)
        EQ = spare(4224, WR * NW)
        SAME = [region(25600 + NW * i, NW) for i in range(2)]
        SAME_W = [region(25600 + NW * (2 + i), NW) for i in range(2)]
        LHS = [region(29696 + P * i, P) for i in range(2)]
        CODE = spare(4224 + 2048, WR * B)
        XQS = sb("xq_now", D)[:, :]
        XQT = [sb(f"xq_turned{i}", D)[:, :] for i in range(2)]

        KG = [region(8192, BW), region(20480, BW)]
        VG = [region(10240, BW), region(22528, BW)]
        KT = [region(12288, BW), region(4096, BW)]
        VT = [region(14336, BW), region(6144, BW)]
        PR = [region(H * KEYS * i, H * KEYS).rearrange("p (h k) -> p h k", k=KEYS) for i in range(2)]
        PT = [region(16384 + 2048 * i, 2048) for i in range(2)]
        QD = [region(24576 + 1024 * i, 1024).rearrange("p (h n) -> p h n", n=P) for i in range(2)]
        VR = [region(26624 + 1024 * i, 1024) for i in range(2)]
        AT = [region(28672 + D * i, D) for i in range(2)]
        R32 = [region(29184 + D * i, D) for i in range(2)]
        Y = [region(29696 + D * i, D) for i in range(2)]
        QS = [region(30208 + D * i, D) for i in range(2)]
        RB = region(30720, D)
        MASK = [region(30976 + KEYS * i, KEYS) for i in range(2)]
        LOWER = region(31328, KEYS)
        NMAX = [region(31504 + H * i, H) for i in range(2)]
        SUMS = [region(31520 + H * i, H) for i in range(2)]

        PS = [ctx.enter_context(nc.psum_tensor(f"bank{i}", [P, 512], F32)) for i in range(8)]

        S_BANK = ((0, 1, 2, 0), (1, 2, 0, 1))
        S_AGO = ((2, 2, 5, 3), (3, 3, 3, 3))
        O_PS, R_PS, Y_PS = PS[6][:, 0:D], PS[7][:, 0:D], PS[7][:, D:2 * D]

        consts_in, ints_in, w_in, wo_in, gain_in, l0_got, l0_kept, l0_first_in, l0_in = (sem(n) for n in (
            "consts_in", "ints_in", "w_in", "wo_in", "gain_in", "l0_got", "l0_kept", "l0_first_in", "l0_in"))
        x_first_in, x_in, cond_in = sem("x_first_in"), sem("x_in"), sem("cond_in")
        dve_step = sem("dve_step")
        spread_rhs, spread_ps, diag_set, rows_ps, rows_set = (sem(n) for n in (
            "spread_rhs", "spread_ps", "diag_set", "rows_ps", "rows_set"))
        win_set, base_set, lhs_set, idx_ps, idx_set = (sem(n) for n in (
            "win_set", "base_set", "lhs_set", "idx_ps", "idx_set"))
        turned, kept_w, angles, sines, cosines, gains, tables_q, tables_k = (sem(n) for n in (
            "turned", "kept_w", "angles", "sines", "cosines", "gains", "tables_q", "tables_k"))
        l0_w_set, w_diag_set, l0_done, x1s_set, x1_kept, x1_turned, x1t_set, kv_done, kv_kept = (sem(n) for n in (
            "l0_w_set", "w_diag_set", "l0_done", "x1s_set", "x1_kept", "x1_turned", "x1t_set", "kv_done", "kv_kept"))
        k_squared, k_summed, k_root, k_inverted, k_scaled_pool, k_scaled, kv_stored = (sem(n) for n in (
            "k_squared", "k_summed", "k_root", "k_inverted", "k_scaled_pool", "k_scaled", "kv_stored"))
        xq_set, xq_turned, xqt_set, q_done, q_kept = (sem(n) for n in (
            "xq_set", "xq_turned", "xqt_set", "q_done", "q_kept"))
        base_in = [sem(f"base_in{j}") for j in range(WR)]
        won_in = [sem(f"won_in{j}") for j in range(WR)]
        laid_k, laid_v, merged_k, merged_v = (sem(n) for n in (
            "laid_k", "laid_v", "merged_k", "merged_v"))
        laid_first, merged_last = sem("laid_first"), sem("merged_last")
        upd_k_stored, upd_v_stored = ([sem(f"upd_{kv}_stored{j}") for j in range(WR)] for kv in "kv")
        q_squared, q_summed, q_root, q_rstd = (sem(n) for n in ("q_squared", "q_summed", "q_root", "q_rstd"))
        k_in = [sem(f"k_in{i}") for i in range(2)]
        v_in = [sem(f"v_in{i}") for i in range(2)]
        kt_set, vt_set, q_scaled, qd_set, mask_set = (sem(n) for n in (
            "kt_set", "vt_set", "q_scaled", "qd_set", "mask_set"))
        scored, masked, probs, p_turned, p_kept, v_turned, v_kept = (sem(n) for n in (
            "scored", "masked", "probs", "p_turned", "p_kept", "v_turned", "v_kept"))
        inverted, r_set, r_spread, r_kept, summed_o, o_scaled, y_done, y_set = (sem(n) for n in (
            "inverted", "r_set", "r_spread", "r_kept", "summed_o", "o_scaled", "y_done", "y_set"))
        y_sent = [sem(f"y_sent{i}") for i in range(2)]

        KEY_CHUNKS = ((0, 8), (8, 16), (16, 24), (24, 28), (28, NT))
        KC = len(KEY_CHUNKS)
        ROOTS = [slice(G * KEY_CHUNKS[a][0], G * KEY_CHUNKS[b - 1][1]) for a, b in ((0, 2), (2, KC - 1), (KC - 1, KC))]
        QC, QN = 8, NT // 8

        def table_parts(cos_tab, sin_tab, g0):
            sin, cos = (a.rearrange("p (j f) -> p j f", f=HALF) for a in (ANG[1], ANG[2]))
            return [(tab[:, :, HALF * half:HALF * (half + 1)], trig,
                     qk_gain[:, g0 + g:g0 + g + HALF].unsqueeze(1).to_broadcast([P, NT, HALF]))
                    for tab, half, trig, g in ((cos_tab, 0, cos, 0), (cos_tab, 1, cos, HALF),
                                               (sin_tab, 0, sin, HD + HALF), (sin_tab, 1, sin, 0))]

        def lay(copy, merge, base, kv, done, *more):
            copy(merge.rearrange("p (o c) -> p o c", o=BLOCK)[:, :, TOK * kv:TOK * (kv + 1)]
                 .rearrange("p o (g d) -> p g o d", g=G),
                 base[kv].rearrange("p (g o d) -> p g o d", g=G, o=BLOCK), *more).then_inc(done, 1)

        def lay_back(copy, base, merge, kv, done, *more):
            copy(base[kv].rearrange("p (g o d) -> p g o d", g=G, o=BLOCK),
                 merge.rearrange("p (o c) -> p o c", o=BLOCK)[:, :, TOK * kv:TOK * (kv + 1)]
                 .rearrange("p o (g d) -> p g o d", g=G), *more).then_inc(done, 1)

        def keys_of_chunk(n):
            a, b = KEY_CHUNKS[n]
            return ROW[:, a:b, 0:TOK]

        def chunk_flat(buf, n):
            a, b = KEY_CHUNKS[n]
            return buf[:, 0:(b - a) * TOK].rearrange("p (j c) -> p j c", c=TOK)

        def chunk_of(buf, n):
            a, b = KEY_CHUNKS[n]
            return buf[:, 0:(b - a) * TOK].rearrange("p (j g d) -> p j g d", g=G, d=HD)

        def scale_keys(engine, n, done):
            a, b = KEY_CHUNKS[n]
            k4 = keys_of_chunk(n).rearrange("p j (g d) -> p j g d", d=HD)
            engine.tensor_tensor(k4, k4, SD_K[:, G * a:G * b].rearrange("p (j g) -> p j g", g=G)
                                 .unsqueeze(3).to_broadcast([P, b - a, G, HD]), ALU.mult).then_inc(done, 1)

        block = ctx.enter_context(nc.Block())

        @block.sync
        def _(sp):
            sp.dma_start(cond_i, cond.rearrange("(b o) -> b o", o=1)).then_inc(cond_in, 16)
            sp.dma_start(kv_i, kv_lens.rearrange("(b o) -> b o", o=1)).then_inc(ints_in, 16)
            sp.dma_start(TBL_I, table).then_inc(ints_in, 16)
            sp.dma_start(CST[:, :], consts).then_inc(consts_in, 16)
            sp.dma_start(W_RAW[:, 0:2, :], wq.rearrange("(o p) d -> p o d", p=P)).then_inc(w_in, 16)
            sp.dma_start(W_RAW[:, 2, :], wk).then_inc(w_in, 16)
            sp.dma_start(W_RAW[:, 3, :], wv).then_inc(w_in, 16)
            sp.wait_ge(l0_got, 16)
            sp.dma_start(l0_rows, Q[:, 0:T * HD]).then_inc(l0_kept, 16)
            x_tiles = x.rearrange("(j s) c t -> (s c) j t", s=TPS)

            def load_x(n):
                sp.dma_start(x3[:, 8 * n:8 * n + 8, :], x_tiles[:, 8 * n:8 * n + 8, :]).then_inc(x_in if n else x_first_in, 16)

            load_x(0)
            sp.wait_ge(l0_kept, 16)
            l0_tiles = l0_rows.rearrange("(j s) (c d) -> (s c) j d", s=TPS, d=HD)
            sp.dma_start(L0_W[:, 0:8, :], l0_tiles[:, 0:8, :]).then_inc(l0_first_in, 16)
            sp.dma_start(L0_W[:, 8:NT, :], l0_tiles[:, 8:NT, :]).then_inc(l0_in, 16)
            sp.dma_start(qk_gain[:, 0:HD], q_scale.rearrange("(o d) -> o d", o=1).to_broadcast([P, HD])).then_inc(gain_in, 16)
            sp.dma_start(qk_gain[:, 2 * HD:3 * HD], k_scale.rearrange("(o d) -> o d", o=1).to_broadcast([P, HD])).then_inc(gain_in, 16)
            for o in range(2):
                for e in range(H2):
                    sp.dma_start(W_RAW[:, 4 + o, P * e:P * (e + 1)].rearrange("p (g d) -> p g d", d=HD),
                                 wo[P * o:P * (o + 1), :].rearrange("p (g e d) -> p e g d", e=H2, d=HD)[:, e]).then_inc(wo_in, 16)
            for n in range(1, 4):
                load_x(n)
            new_rows = new_kv.rearrange("(j p) c -> p j c", p=P)

            def store_new(n, c0, c1):
                a, b = KEY_CHUNKS[n]
                sp.dma_start(new_rows[:, a:b, c0:c1], ROW[:, a:b, c0:c1]).then_inc(kv_stored, 16)

            def store_values(n):
                sp.wait_ge(kv_kept, KEY_CHUNKS[n][1])
                store_new(n, TOK, 2 * TOK)

            for n in range(KC - 1):
                store_values(n)
            for n in range(2):
                sp.wait_ge(k_scaled_pool, n + 1)
                store_new(n, 0, TOK)
            store_values(KC - 1)
            for n in range(2, KC):
                sp.wait_ge(k_scaled, n - 1)
                store_new(n, 0, TOK)
            for i, j in enumerate(ORDER):
                if i < WR - 1:
                    sp.wait_ge(merged_k, i + 1)
                else:
                    sp.wait_ge(merged_last, 1)
                sp.dma_start(upd[0][P * j:P * (j + 1), :], BASE[j][0]).then_inc(upd_k_stored[j], 16)
                if i < WR - 1:
                    sp.wait_ge(merged_v, i + 1)
                else:
                    sp.wait_ge(merged_last, 2)
                sp.dma_start(upd[1][P * j:P * (j + 1), :], BASE[j][1]).then_inc(upd_v_stored[j], 16)
            out_tiles = out.rearrange("(j s) c t -> j (s c) t", s=TPS)
            with sp.Fori(0, NG) as g:
                for b2 in range(2):
                    sp.wait_ge(y_set, 2 * g + b2 + 1)
                    sp.dma_start(out_tiles[bass.ds(2 * g + b2, 1)].rearrange("o p t -> p (o t)"),
                                 Y[b2]).then_inc(y_sent[b2], 16)
            for b2 in range(2):
                sp.wait_ge(y_sent[b2], 16 * NG)

        @block.gpsimd
        def _(pool):
            pool.wait_ge(cond_in, 16)
            pool.indirect_dma_start(Q[:, 0:T * HD], None, l0_w.rearrange("s c d -> s (c d)"),
                                    bass.IndirectOffsetOnAxis(cond_i, 0), bounds_check=CONDS - 1,
                                    oob_is_err=False).then_inc(l0_got, 16)
            pool.wait_ge(l0_first_in, 16)
            pool.wait_ge(consts_in, 16)

            def add_eye(n):
                if n == 1:
                    pool.wait_ge(l0_in, 16)
                pool.tensor_tensor(L0_W[:, 8 * n:8 * n + 8, :], L0_W[:, 8 * n:8 * n + 8, :],
                                   c("eye_t").unsqueeze(1).to_broadcast([P, 8, HD]), ALU.add).then_inc(l0_w_set, 1)
                pool.wait_ge(l0_w_set, n + 1)

            def w_diag(q):
                if q >= 2:
                    pool.wait_ge(l0_done, 4 * (q - 1))
                wide = [P, 4, TPS, HD]
                pool.tensor_tensor(W_DIAG4[q % 2], L0_W[:, 4 * q:4 * q + 4, :].unsqueeze(2).to_broadcast(wide),
                                   c("same_quadrant").rearrange("p (s d) -> p s d", s=TPS).unsqueeze(1).to_broadcast(wide),
                                   ALU.mult).then_inc(w_diag_set, 1)

            def table_q(n):
                pool.tensor_tensor(*table_parts(COS_Q, SIN_Q, 0)[n], ALU.mult).then_inc(tables_q, 1)

            def key_squares(n):
                k = keys_of_chunk(n)
                pool.wait_ge(kv_kept, KEY_CHUNKS[n][1])
                if n:
                    pool.wait_ge(k_summed, n)
                pool.tensor_tensor(chunk_flat(SQ, n), k, k, ALU.mult).then_inc(k_squared, 1)

            def get_base(j):
                for kv, cache in enumerate((k_blocks, v_blocks)):
                    pool.indirect_dma_start(BASE[j][kv], None, cache.rearrange("n g o d -> n (g o d)"),
                                            bass.IndirectOffsetOnAxis(base_idx[:, j:j + 1], 0),
                                            bounds_check=CACHE - 1, oob_is_err=False).then_inc(base_in[j], 16)

            for q in range(8):
                if q % 2 == 0:
                    add_eye(q // 2)
                w_diag(q)
                if q == 1:
                    pool.wait_ge(base_set, 1)
                    get_base(0)
                    get_base(1)
                    pool.wait_ge(cosines, 1)
                    pool.wait_ge(gains, 1)
                if q in (2, 3):
                    table_q(2 * q - 4)
                    table_q(2 * q - 3)
                if q == 4:
                    pool.wait_ge(kept_w, 5)
                    pool.wait_ge(tables_k, 4)
                    pool.wait_ge(tables_q, 4)
                    get_base(2)
                if q == 5:
                    key_squares(0)
            for n in range(1, KC - 1):
                key_squares(n)
            pool.wait_ge(k_inverted, 1)
            for n in range(2):
                scale_keys(pool, n, k_scaled_pool)

            def gather_cache(g, buf, got, cache):
                pool.indirect_dma_start(buf[g % 2], None, cache.rearrange("n g o d -> n (g o d)"),
                                        bass.IndirectOffsetOnAxis(idx_cache[:, g:g + 1], 0),
                                        bounds_check=CACHE - 1, oob_is_err=False).then_inc(got[g % 2], 16)

            keys, values = (KG, k_in, k_blocks, upd[0]), (VG, v_in, v_blocks, upd[1])
            pool.wait_ge(win_set, 1)
            pool.wait_ge(kv_stored, 16 * 2 * KC)
            for i, j in enumerate(ORDER):
                if i:
                    pool.wait_ge(laid_k, i)
                    pool.wait_ge(laid_v, i)
                else:
                    pool.wait_ge(laid_first, 2)
                for o in range(BLOCK):
                    pool.indirect_dma_start(MERGE[j][:, 2 * TOK * o:2 * TOK * (o + 1)], None, new_kv,
                                            bass.IndirectOffsetOnAxis(win_idx[:, BLOCK * j + o:BLOCK * j + o + 1], 0),
                                            bounds_check=B * T - 1, oob_is_err=False).then_inc(won_in[j], 16)
                if i >= 1:
                    if i == 1:
                        pool.wait_ge(idx_set, 2)
                        pool.wait_ge(upd_k_stored[ORDER[0]], 16)
                        pool.wait_ge(upd_v_stored[ORDER[0]], 16)
                    gather_cache(i - 1, *keys[:3])
                    gather_cache(i - 1, *values[:3])

            def gather_new(g, buf, got, new):
                pool.wait_ge(got[g % 2], 32 * (g // 2) + 16)
                pool.indirect_dma_start(buf[g % 2], None, new,
                                        bass.IndirectOffsetOnAxis(idx_upd[:, g:g + 1], 0),
                                        bounds_check=NW - 1, oob_is_err=False).then_inc(got[g % 2], 16)

            def scale_q(n):
                pool.tensor_tensor(QS[n % 2].rearrange("p (h d) -> p h d", d=HD),
                                   q3[:, n, :].rearrange("p (h d) -> p h d", d=HD),
                                   RSTD_Q[:, H * n:H * (n + 1)].unsqueeze(2).to_broadcast([P, H, HD]),
                                   ALU.mult).then_inc(q_scaled, 1)

            pool.wait_ge(q_rstd, QC)
            scale_q(0)
            scale_q(1)
            for g in range(2):
                for what, stored in ((keys, upd_k_stored), (values, upd_v_stored)):
                    if g == 0:
                        for j in range(WR):
                            pool.wait_ge(stored[j], 16)
                    gather_new(g, what[0], what[1], what[3])
            def asked(n):
                return n // 2 + 2, (keys, values)[n % 2]

            for n in range(NT - 2):
                if n >= 2:
                    g, (buf, got, cache, new) = asked(n - 2)
                    if g < NG:
                        gather_new(g, buf, got, new)
                g, (buf, got, cache, new) = asked(n)
                if g < NG:
                    if n % 2 == 0:
                        pool.wait_ge(kt_set, n + 2)
                    else:
                        pool.wait_ge(vt_set, n + 1)
                    gather_cache(g, buf, got, cache)
                pool.wait_ge(qd_set, n + 1)
                scale_q(n + 2)

        @block.vector
        def _(dve):
            steps = [0]

            def link(ins):
                steps[0] += 1
                ins.then_inc(dve_step, 1)
                dve.wait_ge(dve_step, steps[0])

            dve.wait_ge(ints_in, 32)
            link(dve.tensor_scalar(a_i, kv_i, 4, None, ALU.arith_shift_right))
            dve.tensor_copy(kv_f, kv_i).then_inc(dve_step, 1)
            dve.tensor_copy(TBL, TBL_I).then_inc(dve_step, 1)
            steps[0] += 2
            link(dve.tensor_copy(a_f, a_i))
            dve.wait_ge(consts_in, 16)
            dve.tensor_scalar(by_tile[:, 0:NT], c("in_tile"), kv_f, None, ALU.mult).then_inc(spread_rhs, 1)
            dve.tensor_scalar(by_tile[:, NT:2 * NT], c("in_tile"), a_f, None, ALU.mult).then_inc(spread_rhs, 1)
            link(dve.scalar_tensor_tensor(r_f, a_f, -float(BLOCK), kv_f, ALU.mult, ALU.add))
            link(dve.tensor_scalar(slot_no, c("slot"), a_f, -float(BACK), ALU.add, ALU.add))
            link(dve.tensor_scalar(slot_no, slot_no, 0.0, float(NBLK - 1), ALU.max, ALU.min))
            link(dve.memset(blk, SKIP))
            for s in range(SLOTS):
                dve.scalar_tensor_tensor(MATCHES[:, NBLK * s:NBLK * (s + 1)], c("column"), slot_no[:, s:s + 1], TBL,
                                         ALU.is_equal, ALU.mult, accum_out=blk[:, s:s + 1]).then_inc(dve_step, 1)
            steps[0] += SLOTS
            dve.wait_ge(dve_step, steps[0])
            for j in range(WR):
                dve.tensor_scalar(DIAG[:, B * j:B * (j + 1)], c("ident"), blk[:, BACK + SPREAD[j]:BACK + SPREAD[j] + 1], None,
                                  ALU.mult).then_inc(diag_set, 1)
            dve.tensor_scalar(DIAG[:, NW:NW + B], c("ident"), r_f, None, ALU.mult).then_inc(diag_set, 1)
            dve.tensor_copy(base_idx, blk[:, BACK:BACK + WR]).then_inc(base_set, 1)
            dve.wait_ge(spread_ps, 1)
            link(dve.tensor_scalar(pos, PS[6][:, 0:NT], c("t"), None, ALU.add))
            link(dve.scalar_tensor_tensor(hi, PS[6][:, NT:2 * NT], -float(BLOCK), pos, ALU.mult, ALU.add))
            link(dve.tensor_scalar(lo, hi, -float(WINDOW - 1), None, ALU.add))
            link(dve.scalar_tensor_tensor(lo, PS[6][:, NT:2 * NT], -float(BLOCK), lo, ALU.mult, ALU.max))
            link(dve.tensor_scalar(hi, hi, BIG, None, ALU.mult))
            link(dve.tensor_scalar(lo, lo, BIG, None, ALU.mult))
            a0, a1, a2 = ANG
            grid = lambda a: a.rearrange("p (j f) -> p j f", f=HALF)
            link(dve.tensor_tensor(grid(a0), pos.unsqueeze(2).to_broadcast([P, NT, HALF]),
                                   c("inv_freq").unsqueeze(1).to_broadcast([P, NT, HALF]), ALU.mult))
            link(dve.tensor_scalar(a1, a0, float(1 / (2 * np.pi)), ROUND, ALU.mult, ALU.add))
            link(dve.tensor_scalar(a1, a1, ROUND, None, ALU.subtract))
            for part in (TWO_PI_A, TWO_PI_B, TWO_PI_C):
                link(dve.scalar_tensor_tensor(a0, a1, -part, a0, ALU.mult, ALU.add))
            dve.tensor_scalar(a0, a0, PI_IN, -PI_IN, ALU.min, ALU.max).then_inc(angles, 1)
            dve.wait_ge(gain_in, 32)
            link(dve.tensor_scalar(qk_gain[:, 0:HD], qk_gain[:, 0:HD], 1.0, -SCALE, ALU.add, ALU.mult))
            link(dve.tensor_scalar(qk_gain[:, HD:2 * HD], qk_gain[:, 0:HD], -1.0, None, ALU.mult))
            link(dve.tensor_scalar(qk_gain[:, 2 * HD:3 * HD], qk_gain[:, 2 * HD:3 * HD], 1.0, None, ALU.add))
            dve.tensor_scalar(qk_gain[:, 3 * HD:4 * HD], qk_gain[:, 2 * HD:3 * HD], -1.0, None, ALU.mult).then_inc(gains, 1)
            dve.wait_ge(sines, 2)
            link(dve.tensor_tensor(a2, a2, a2, ALU.mult))
            dve.tensor_scalar(a2, a2, -2.0, 1.0, ALU.mult, ALU.add).then_inc(cosines, 1)
            dve.wait_ge(cosines, 1)
            for part in table_parts(COS_K, SIN_K, 2 * HD):
                dve.tensor_tensor(*part, ALU.mult).then_inc(tables_k, 1)
            dve.wait_ge(rows_set, 1)
            per_off = [P, BLOCK, B]
            r_row = ROWS[:, NW:NW + B]
            codes = [CODE[:, B * j:B * (j + 1)] for j in range(WR)]
            dve.tensor_tensor(COVERS, c("off").unsqueeze(2).to_broadcast(per_off),
                              r_row.unsqueeze(1).to_broadcast(per_off), ALU.is_ge).then_inc(dve_step, 1)
            steps[0] += 1
            link(dve.tensor_tensor(codes[0], c("first_code"), r_row, ALU.subtract))
            for j in (1, 2):
                dve.tensor_scalar(codes[j], codes[0], float(BLOCK * j), None, ALU.add).then_inc(dve_step, 1)
            steps[0] += 2
            dve.wait_ge(dve_step, steps[0])
            dve.tensor_tensor(CAND[:, :, 0, :], COVERS, codes[0].unsqueeze(1).to_broadcast(per_off), ALU.mult).then_inc(dve_step, 1)
            steps[0] += 1
            link(dve.scalar_tensor_tensor(CAND[:, :, 1, :], COVERS, 0.0, codes[2].unsqueeze(1).to_broadcast(per_off),
                                          ALU.is_equal, ALU.mult))
            for j in range(WR):
                dve.tensor_scalar(EQ[:, NW * j:NW * (j + 1)], ROWS[:, 0:NW], blk[:, BACK + j:BACK + j + 1], None,
                                  ALU.is_equal).then_inc(dve_step, 1)
            steps[0] += WR
            dve.wait_ge(dve_step, steps[0])
            first = steps[0]

            def last_writer(n, same, codes_, to):
                if n >= len(JUNK):
                    dve.wait_ge(dve_step, first + n - len(JUNK) + 1)
                dve.tensor_tensor_reduce(out=JUNK[n % len(JUNK)][:, 0:codes_.shape[-1]], in0=same, in1=codes_, scale=1.0,
                                         scalar=0.0, op0=ALU.mult, op1=ALU.max, accum_out=to).then_inc(dve_step, 1)

            for j in range(WR):
                for o in range(BLOCK):
                    last_writer(BLOCK * j + o, EQ[:, NW * j:NW * j + 2 * B], CAND[:, o, :, :].rearrange("p j b -> p (j b)"),
                                won[:, BLOCK * j + o:BLOCK * j + o + 1])
            for j in range(WR):
                last_writer(WR * BLOCK + j, EQ[:, NW * j + 2 * B:NW * (j + 1)], codes[1], won_whole[:, j:j + 1])
            steps[0] = first + WR * (BLOCK + 1)
            dve.wait_ge(dve_step, steps[0])
            won3 = won.rearrange("p (j o) -> p j o", o=BLOCK)
            link(dve.tensor_tensor(won3, won3, won_whole.unsqueeze(2).to_broadcast([P, WR, BLOCK]), ALU.max))
            nobody = JUNK[0][:, 0:WR * BLOCK]
            link(dve.tensor_scalar(nobody, won, 0.0, SKIP, ALU.is_equal, ALU.mult))
            link(dve.tensor_tensor(won3, won3, c("off").unsqueeze(1).to_broadcast([P, WR, BLOCK]), ALU.add))
            dve.scalar_tensor_tensor(win_idx, won, -float(BLOCK + 1), nobody, ALU.add, ALU.add).then_inc(win_set, 1)
            dve.wait_ge(win_set, 1)

            def invert_roots(n):
                dve.wait_ge(k_root, n + 1)
                dve.reciprocal(SD_K[:, ROOTS[n]], SD_K[:, ROOTS[n]]).then_inc(k_inverted, 1)

            for n, (a, b) in enumerate(KEY_CHUNKS):
                if n == 3:
                    invert_roots(0)
                k4 = keys_of_chunk(n).rearrange("p j (g d) -> p j g d", d=HD)
                ta, tb = chunk_of(TA, n), chunk_of(TB, n)
                dve.wait_ge(kv_kept, b)
                dve.tensor_tensor(ta, k4, COS_K[:, a:b, :].unsqueeze(2).to_broadcast([P, b - a, G, HD]),
                                  ALU.mult).then_inc(dve_step, 1)
                for half in range(2):
                    dve.tensor_tensor(tb[:, :, :, HALF * half:HALF * (half + 1)],
                                      k4[:, :, :, HALF * (1 - half):HALF * (2 - half)],
                                      SIN_K[:, a:b, HALF * half:HALF * (half + 1)].unsqueeze(2)
                                      .to_broadcast([P, b - a, G, HALF]), ALU.mult).then_inc(dve_step, 1)
                steps[0] += 3
                dve.wait_ge(k_squared, n + 1)
                dve.tensor_reduce(SS_K[:, G * a:G * b], SQ[:, 0:(b - a) * TOK].rearrange("p (h d) -> p h d", d=HD), AX.X,
                                  ALU.add).then_inc(k_summed, 1)
                dve.wait_ge(dve_step, steps[0])
                link(dve.tensor_tensor(k4, ta, tb, ALU.add))
            invert_roots(1)
            dve.wait_ge(k_inverted, 2)
            for n in range(2, KC - 1):
                scale_keys(dve, n, k_scaled)
            invert_roots(2)
            dve.wait_ge(k_inverted, 3)
            scale_keys(dve, KC - 1, k_scaled)

            for s in range(SLOTS):
                same = SAME[s % 2]
                link(dve.tensor_scalar(same, ROWS[:, 0:NW], blk[:, s:s + 1], None, ALU.is_equal))
                dve.tensor_tensor_reduce(out=SAME_W[s % 2], in0=same, in1=c("writer"), scale=1.0, scalar=0.0,
                                         op0=ALU.mult, op1=ALU.max, accum_out=match[:, s:s + 1]).then_inc(dve_step, 1)
                steps[0] += 1
            dve.wait_ge(dve_step, steps[0])
            link(dve.tensor_scalar(miss, match, 0.0, SKIP, ALU.is_gt, ALU.mult))
            link(dve.tensor_tensor(blk[:, 0:SLOTS], blk[:, 0:SLOTS], miss, ALU.add))
            lhs = [a.rearrange("p (s k) -> p s k", k=PADDED) for a in LHS]
            place = c("seq_of_slot").unsqueeze(2).to_broadcast([P, 8, PADDED])
            link(dve.tensor_tensor(lhs[0], blk.unsqueeze(1).to_broadcast([P, 8, PADDED]), place, ALU.mult))
            link(dve.tensor_scalar(miss, match, 0.0, SKIP, ALU.is_equal, ALU.mult))
            link(dve.scalar_tensor_tensor(blk[:, 0:SLOTS], match, -1.0, miss, ALU.add, ALU.add))
            dve.tensor_tensor(lhs[1], blk.unsqueeze(1).to_broadcast([P, 8, PADDED]), place, ALU.mult).then_inc(lhs_set, 1)

            unit = dve.alloc_register("units_scored")
            dve.reg_mov(unit, 0)

            def spread_q(n, b2):
                dve.wait_ge(q_scaled, n + 1)
                for rg in range(TPS):
                    ins = dve.transpose(QD[b2][T * rg:T * (rg + 1), :, T * rg:T * (rg + 1)],
                                        QS[b2][T * rg:T * (rg + 1), :].rearrange("p (h d) -> p h d", d=HD))
                ins.then_inc(qd_set, 1)

            def mask_lower(n):
                dve.tensor_scalar(LOWER, c("neg_dist"), lo[:, bass.ds(n, 1)], 0.0, ALU.add, ALU.max).then_inc(mask_set, 1)

            def mask(n, b2):
                dve.wait_ge(mask_set, 2 * n + 1)
                dve.scalar_tensor_tensor(MASK[b2], c("dist"), hi[:, bass.ds(n, 1)], LOWER, ALU.subtract, ALU.max).then_inc(mask_set, 1)

            base = steps[0]

            def rotate_q(n):
                tiles = bass.ds(QN * n, QN)
                qt = q3[:, tiles, :].rearrange("p j (h d) -> p j h d", d=HD)
                ta, tb = (a.rearrange("p (j h d) -> p j h d", j=QN, h=H) for a in (TA, TB))
                wide = [P, QN, H, HD]
                dve.wait_ge(q_squared, n + 1)
                dve.tensor_reduce(ss, SQ.rearrange("p (h d) -> p h d", d=HD), AX.X, ALU.add).then_inc(q_summed, 1)
                dve.tensor_tensor(ta, qt, COS_Q[:, tiles, :].unsqueeze(2).to_broadcast(wide), ALU.mult).then_inc(dve_step, 1)
                for half in range(2):
                    dve.tensor_tensor(tb[:, :, :, HALF * half:HALF * (half + 1)],
                                      qt[:, :, :, HALF * (1 - half):HALF * (2 - half)],
                                      SIN_Q[:, tiles, HALF * half:HALF * (half + 1)].unsqueeze(2).to_broadcast([P, QN, H, HALF]),
                                      ALU.mult).then_inc(dve_step, 1)
                dve.wait_ge(dve_step, base + 4 * n + 3)
                dve.tensor_tensor(qt, ta, tb, ALU.add).then_inc(dve_step, 1)
                dve.wait_ge(q_root, n + 1)
                dve.reciprocal(RSTD_Q[:, bass.ds(QN * H * n, QN * H)], sd).then_inc(q_rstd, 1)
                dve.wait_ge(dve_step, base + 4 * n + 4)

            dve.wait_ge(tables_q, 4)
            dve.wait_ge(kv_stored, 16 * 2 * KC)
            for j in ORDER[1:]:
                dve.wait_ge(base_in[j], 32)
                lay(dve.tensor_copy, MERGE[j], BASE[j], 1, laid_v)

            def merge_v(j):
                dve.wait_ge(won_in[j], 16 * BLOCK)
                lay_back(dve.tensor_copy, BASE[j], MERGE[j], 1, merged_v)

            for (a, b), j in zip(((0, 2), (2, 5), (5, QC)), ORDER):
                with dve.Fori(a, b) as n:
                    rotate_q(n)
                if a == 0:
                    dve.wait_ge(idx_ps, 1)
                    dve.tensor_copy(idx_cache, PS[6][:, 0:NG]).then_inc(idx_set, 1)
                    dve.tensor_copy(idx_upd, PS[6][:, NG:2 * NG]).then_inc(idx_set, 1)
                if b < QC:
                    merge_v(j)
                else:
                    steps[0] = base + 4 * QC
                    for b2 in range(2):
                        link(dve.memset(QD[b2], 0.0))
                    mask_lower(0)
                    mask(0, 0)
                    spread_q(0, 0)

            def turn(buf, turned, got, done, g, p, half):
                dve.wait_ge(got[p], 16 * (g - p) + 32)
                cols = slice(BW // 2 * half, BW // 2 * (half + 1))
                dve.transpose(turned[p][:, cols].rearrange("p (g k o) -> p g o k", g=G // 2, o=BLOCK),
                              buf[p][:, cols].rearrange("p (g o d) -> p g o d", g=G // 2, d=HD)).then_inc(done, 1)

            def lower(n, b2, g):
                dve.wait_ge(mask_set, 2 * n + 2)
                dve.reg_add(unit, unit, 1)
                dve.wait_ge(merged_v, WR - 1)
                dve.wait_ge(scored, unit)
                for h2 in range(H2):
                    h = H2 * g + h2
                    dve.tensor_tensor_reduce(out=PR[b2][:, h, :], in0=PS[S_BANK[b2][g]][:, KEYS * h2:KEYS * (h2 + 1)],
                                             in1=MASK[b2], scale=1.0, scalar=HUGE, op0=ALU.add, op1=ALU.min,
                                             accum_out=NMAX[b2][:, h:h + 1]).then_inc(masked, 1)

            def invert(n, b2):
                dve.wait_ge(probs, 8 * n + 8)
                dve.reciprocal(SUMS[b2], SUMS[b2]).then_inc(inverted, 1)

            def repeat_r(n, b2):
                dve.wait_ge(inverted, n + 1)
                dve.tensor_copy(R32[b2].rearrange("p (e g d) -> p e g d", e=H2, g=G),
                                SUMS[b2].rearrange("p (g e) -> p e g", e=H2).unsqueeze(3)
                                .to_broadcast([P, H2, G, HD])).then_inc(r_set, 1)

            def scale_o(n, b2):
                dve.wait_ge(summed_o, n + 1)
                dve.wait_ge(r_kept, n + 1)
                dve.tensor_tensor(AT[b2], O_PS, RB, ALU.mult).then_inc(o_scaled, 1)

            def add_res(n, b2, sent):
                dve.wait_ge(y_done, n + 1)
                if sent is not None:
                    dve.wait_ge(y_sent[b2], sent)
                dve.tensor_tensor(Y[b2], Y_PS, X[:, bass.ds(D * n, D)], ALU.add).then_inc(y_set, 1)

            def stage(n, m, i):
                b2, p, loop = m % 2, m // 2 % 2, not isinstance(n, int)
                new, prev, old = loop or n < NT, loop or 1 <= n <= NT, loop or 2 <= n < NT + 2
                g = 2 * i + p
                more = loop or (new and (b2 == 0 or g + 1 < NG))
                if new:
                    lower(n, b2, 0)
                if loop or n >= 3:
                    sent = 16 * (g - 2 if b2 == 0 else g - 1)
                    add_res(n - 3, 1 - b2, sent if loop or n >= 5 else None)
                if loop or n + 1 < NT:
                    mask_lower(n + 1)
                    spread_q(n + 1, 1 - b2)
                if new:
                    lower(n, b2, 1)
                if prev:
                    invert(n - 1, 1 - b2)
                if loop or n + 1 < NT:
                    mask(n + 1, 1 - b2)
                if prev:
                    repeat_r(n - 1, 1 - b2)
                turn_args = ((VG, VT, v_in, vt_set, g, p), (KG, KT, k_in, kt_set, g + 1, 1 - p))[b2]
                if more:
                    turn(*turn_args, 0)
                if new:
                    lower(n, b2, 2)
                if old:
                    scale_o(n - 2, b2)
                if new:
                    lower(n, b2, 3)
                if more:
                    turn(*turn_args, 1)

            for half in range(2):
                turn(KG, KT, k_in, kt_set, 0, 0, half)
            for n in range(4):
                stage(n, n, 0)
            with dve.Fori(1, NT // 4 - 1) as i:
                for m in range(4):
                    stage(4 * i + m, m, i)
            for n in range(NT - 4, NT + 3):
                stage(n, n % 4, n // 4)

        @block.scalar
        def _(act):
            act.wait_ge(rows_ps, 1)
            act.activation(ROWS, PS[7][:, :], ACT.Copy).then_inc(rows_set, 1)
            for half in range(2):
                act.wait_ge(turned, half + 1)
                act.activation(WQ_T[:, D * half:D * (half + 1)], PS[half][:, 0:D], ACT.Copy).then_inc(kept_w, 1)
                act.activation(W_KV[:, half, :], PS[half][:, D:2 * D], ACT.Copy).then_inc(kept_w, 1)
            act.wait_ge(angles, 1)
            act.activation(ANG[1], ANG[0], ACT.Sin).then_inc(sines, 1)
            act.activation(ANG[2], ANG[0], ACT.Sin, scale=0.5).then_inc(sines, 1)

            def stage_x1(j, slot):
                act.wait_ge(l0_done, j + 1)
                act.activation(X1S[slot], PS[slot][:, 0:D], ACT.Copy).then_inc(x1s_set, 1)

            def keep_x1(j, slot):
                act.activation(X[:, bass.ds(D * j, D)], PS[slot][:, 0:D], ACT.Copy).then_inc(x1_kept, 1)

            def turned_x1(j, slot):
                act.wait_ge(x1_turned, j + 1)
                act.activation(X1T[slot], PS[2 + slot][:, 0:D], ACT.Copy).then_inc(x1t_set, 1)

            def keep_kv(j, slot):
                act.wait_ge(kv_done, j + 1)
                act.activation(ROW[:, bass.ds(j, 1), :].rearrange("p o c -> p (o c)"), PS[4 + slot][:, 0:D],
                               ACT.Copy).then_inc(kv_kept, 1)

            def root_keys(n, summed):
                act.wait_ge(k_summed, summed)
                act.activation(SD_K[:, ROOTS[n]], SS_K[:, ROOTS[n]], ACT.Sqrt, bias=c("eps"), scale=1.0 / HD).then_inc(k_root, 1)

            def tiles8(k):
                for u in range(8):
                    j, slot = 8 * k + u, u % 2
                    static = isinstance(k, int)
                    if static and j == ROOT_AT:
                        root_keys(0, 2)
                    turned_x1(j, slot)
                    if not static or j + 1 < NT:
                        stage_x1(j + 1, 1 - slot)
                        keep_x1(j + 1, 1 - slot)
                    if not static or j:
                        keep_kv(j - 1, 1 - slot)

            ROOT_AT = NT - 3
            stage_x1(0, 0)
            keep_x1(0, 0)
            tiles8(0)
            act.wait_ge(turned, 3)
            act.activation(WO_T[:, :], PS[7][:, :], ACT.Copy).then_inc(kept_w, 1)
            with act.Fori(1, NT // 8 - 1) as k:
                tiles8(k)
            tiles8(NT // 8 - 1)
            keep_kv(NT - 1, 1)

            act.wait_ge(k_summed, KC - 1)
            act.wait_ge(kv_kept, NT)
            act.activation(chunk_flat(SQ, KC - 1), keys_of_chunk(KC - 1), ACT.Square).then_inc(k_squared, 1)
            root_keys(1, KC - 1)
            root_keys(2, KC)
            act.wait_ge(base_in[ORDER[0]], 32)
            act.wait_ge(kv_done, NT)
            for kv in range(2):
                lay(act.activation, MERGE[ORDER[0]], BASE[ORDER[0]], kv, laid_first, ACT.Copy)

            def stage_xq(j):
                act.activation(XQS, X[:, bass.ds(D * j, D)], ACT.Copy).then_inc(xq_set, 1)

            def turned_xq(j, slot):
                act.wait_ge(xq_turned, j + 1)
                act.activation(XQT[slot], PS[2 + slot][:, 0:D], ACT.Copy).then_inc(xqt_set, 1)

            def keep_q(j, slot):
                act.wait_ge(q_done, j + 1)
                act.activation(Q[:, bass.ds(D * j, D)], PS[4 + slot][:, 0:D], ACT.Copy).then_inc(q_kept, 1)

            def root_q(n):
                act.wait_ge(q_summed, n + 1)
                act.activation(sd, ss, ACT.Sqrt, bias=c("eps"), scale=1.0 / HD).then_inc(q_root, 1)

            def chunk_q(n):
                static = isinstance(n, int)
                for u in range(QN):
                    j, slot = QN * n + u, u % 2
                    turned_xq(j, slot)
                    if not static or j + 1 < NT:
                        stage_xq(j + 1)
                    if not static or j:
                        keep_q(j - 1, 1 - slot)
                    if u == 0 and (not static or n):
                        square_q(n - 1)

            def square_q(n):
                if not isinstance(n, int) or n:
                    root_q(n - 1)
                act.wait_ge(q_kept, QN * n + QN)
                act.activation(SQ, Q[:, bass.ds(QN * D * n, QN * D)], ACT.Square).then_inc(q_squared, 1)

            def merge_k(j):
                act.wait_ge(won_in[j], 16 * BLOCK)
                lay_back(act.activation, BASE[j], MERGE[j], 0, merged_k, ACT.Copy)

            act.wait_ge(x1_kept, NT)
            act.wait_ge(win_set, 1)
            stage_xq(0)
            chunk_q(0)
            act.wait_ge(kv_stored, 16 * 2 * KC)
            for j in ORDER[1:]:
                act.wait_ge(base_in[j], 32)
                lay(act.activation, MERGE[j], BASE[j], 0, laid_k, ACT.Copy)
            chunk_q(1)
            for (a, b), j in zip(((2, 3), (3, 6)), ORDER):
                if b - a == 1:
                    chunk_q(a)
                else:
                    with act.Fori(a, b) as n:
                        chunk_q(n)
                merge_k(j)
            with act.Fori(6, QC - 1) as n:
                chunk_q(n)
            chunk_q(QC - 1)
            keep_q(NT - 1, 1)
            square_q(QC - 1)
            j = ORDER[2]
            act.wait_ge(won_in[j], 16 * BLOCK)
            for kv in range(2):
                lay_back(act.activation, BASE[j], MERGE[j], kv, merged_last, ACT.Copy)
            root_q(QC - 1)

            def exps(n, b2, g):
                for h2 in range(H2):
                    h = H2 * g + h2
                    act.wait_ge(masked, 8 * n + h + 1)
                    act.activation(PR[b2][:, h, :], PR[b2][:, h, :], ACT.Exp, bias=NMAX[b2][:, h:h + 1], scale=-1.0,
                                   accum_out=SUMS[b2][:, h:h + 1]).then_inc(probs, 1)

            def keep_p(n, b2, g):
                act.wait_ge(p_turned, 4 * n + g + 1)
                act.activation(PT[b2][0:CH, 512 * g:512 * (g + 1)], PS[3 + g % 2][0:CH, :], ACT.Copy).then_inc(p_kept, 1)

            def keep_v(n, b2, ch):
                act.wait_ge(v_turned, 2 * n + ch + 1)
                act.activation(VR[b2][0:CH, 512 * ch:512 * (ch + 1)], PS[5][0:CH, :], ACT.Copy).then_inc(v_kept, 1)

            def keep_r(n):
                act.wait_ge(r_spread, n + 1)
                act.activation(RB, R_PS, ACT.Copy).then_inc(r_kept, 1)

            def stage(n, m):
                b2, loop = m % 2, not isinstance(n, int)
                new, prev, old = loop or n < NT, loop or 1 <= n <= NT, loop or 2 <= n < NT + 2
                for g in range(G):
                    if new and g < 3:
                        exps(n, b2, g)
                    if old and g == 1:
                        keep_r(n - 2)
                    if prev and g in (1, 3):
                        keep_v(n - 1, 1 - b2, int(g == 3))
                    if prev:
                        keep_p(n - 1, 1 - b2, g)
                if new:
                    exps(n, b2, 3)

            for n in range(4):
                stage(n, n)
            with act.Fori(1, NT // 4) as i:
                for m in range(4):
                    stage(4 * i + m, m)
            for n in range(NT, NT + 2):
                stage(n, n % 4)

        @block.tensor
        def _(pe):
            ident = c("ident")
            pe.wait_ge(consts_in, 16)
            pe.wait_ge(spread_rhs, 2)
            pe.matmul(PS[6][:, 0:2 * NT], c("token_of_seq"), by_tile, start=True, stop=True).then_inc(spread_ps, 1)
            pe.wait_ge(diag_set, 4)
            pe.matmul(PS[7][:, :], c("ones"), DIAG, start=True, stop=True).then_inc(rows_ps, 1)
            pe.wait_ge(w_in, 16 * 3)
            for half in range(2):
                for o in range(4):
                    ins = pe.transpose(PS[half][:, P * o:P * (o + 1)], W_RAW[:, o, P * half:P * (half + 1)], ident)
                ins.then_inc(turned, 1)

            def layer0(k, u):
                if isinstance(k, int) and 8 * k + u == 8:
                    pe.wait_ge(x_in, 48)
                if u % 4 == 0:
                    pe.wait_ge(w_diag_set, 2 * k + u // 4 + 1)
                pe.matmul(PS[u % 2][:, 0:D], W_DIAG[u % 8], X[:, bass.ds(D * (8 * k + u), D)], start=True, stop=True).then_inc(l0_done, 1)

            def project_kv(slot):
                for half in range(2):
                    ins = pe.matmul(PS[4 + slot][:, 0:D], X1T[slot][:, P * half:P * (half + 1)], W_KV[:, half, :],
                                    start=(half == 0), stop=(half == 1))
                ins.then_inc(kv_done, 1)

            def tiles8(k):
                for u in range(8):
                    j, slot = 8 * k + u, u % 2
                    pe.wait_ge(x1s_set, j + 1)
                    for half in range(2):
                        ins = pe.transpose(PS[2 + slot][:, P * half:P * (half + 1)], X1S[slot][:, P * half:P * (half + 1)], ident)
                    ins.then_inc(x1_turned, 1)
                    if not isinstance(k, int) or j + 1 < NT:
                        layer0(k, u + 1)
                    if not isinstance(k, int) or j:
                        project_kv(1 - slot)

            pe.wait_ge(kept_w, 4)
            pe.wait_ge(x_first_in, 16)
            layer0(0, 0)
            tiles8(0)
            pe.wait_ge(wo_in, 16 * 4)
            pe.wait_ge(rows_set, 1)
            for e in range(H2):
                for o in range(2):
                    ins = pe.transpose(PS[7][:, D * e + P * o:D * e + P * (o + 1)],
                                       W_RAW[:, 4 + o, P * e:P * (e + 1)], ident)
            ins.then_inc(turned, 1)
            with pe.Fori(1, NT // 8 - 1) as k:
                tiles8(k)
            tiles8(NT // 8 - 1)
            pe.wait_ge(x1t_set, NT)
            project_kv(1)

            def turn_xq(j, slot):
                pe.wait_ge(xq_set, j + 1)
                for half in range(2):
                    ins = pe.transpose(PS[2 + slot][:, P * half:P * (half + 1)], XQS[:, P * half:P * (half + 1)], ident)
                ins.then_inc(xq_turned, 1)

            def project_q(slot):
                for half in range(2):
                    ins = pe.matmul(PS[4 + slot][:, 0:D], XQT[slot][:, P * half:P * (half + 1)],
                                    WQ_T[:, D * half:D * (half + 1)], start=(half == 0), stop=(half == 1))
                ins.then_inc(q_done, 1)

            turn_xq(0, 0)
            turn_xq(1, 1)
            project_q(0)
            for a, b in ((1, 4), (4, NT // 2)):
                with pe.Fori(a, b) as i:
                    for u in range(2):
                        turn_xq(2 * i + u, u)
                        project_q(1 - u)
                if a == 1:
                    pe.wait_ge(lhs_set, 1)
                    for i in range(2):
                        ins = pe.matmul(PS[6][:, NG * i:NG * (i + 1)], LHS[i], c("in_group"), start=True, stop=True)
                    ins.then_inc(idx_ps, 1)
            pe.wait_ge(xqt_set, NT)
            project_q(1)

            def keys_of(buf, g, b2):
                return buf[:, 512 * g + 256 * b2:512 * g + 256 * b2 + KEYS]

            def score(n, b2, p, g):
                ago = S_AGO[b2][g]
                if not isinstance(n, int) or 4 * n + g >= ago:
                    pe.wait_ge(masked, 8 * n + 2 * (g - ago + 1))
                for h2 in range(H2):
                    ins = pe.matmul(PS[S_BANK[b2][g]][:, KEYS * h2:KEYS * (h2 + 1)], QD[b2][:, H2 * g + h2, :],
                                    keys_of(KT[p], g, b2), start=True, stop=True)
                ins.then_inc(scored, 1)

            def turn_v(n, b2, p, ch):
                if not isinstance(n, int) or 2 * n + ch >= 1:
                    pe.wait_ge(v_kept, 2 * n + ch)
                for g in range(G):
                    ins = pe.transpose(PS[5][0:CH, P * g:P * (g + 1)],
                                       keys_of(VT[p], g, b2)[:, CH * ch:CH * (ch + 1)], ident)
                ins.then_inc(v_turned, 1)

            def turn_p(n, b2, g):
                if not isinstance(n, int) or 4 * n + g >= 2:
                    pe.wait_ge(p_kept, 4 * n + g - 1)
                pe.wait_ge(probs, 8 * n + 2 * g + 2)
                for ch in range(2):
                    for h2 in range(H2):
                        at_ = P * (H2 * ch + h2)
                        ins = pe.transpose(PS[3 + g % 2][0:CH, at_:at_ + P],
                                           PR[b2][:, H2 * g + h2, CH * ch:CH * (ch + 1)], ident)
                ins.then_inc(p_turned, 1)

            def attend(n, b2):
                if not isinstance(n, int) or n >= 1:
                    pe.wait_ge(o_scaled, n)
                pe.wait_ge(p_kept, 4 * n + 4)
                pe.wait_ge(v_kept, 2 * n + 2)
                o_ps = O_PS.rearrange("p (e t) -> p e t", e=H2)
                for rg in range(TPS):
                    for ch in range(2):
                        for g in range(G):
                            ins = pe.matmul(
                                o_ps[HD * g:HD * (g + 1), :, T * rg:T * (rg + 1)],
                                VR[b2][0:CH, 512 * ch + P * g + HD * rg:512 * ch + P * g + HD * (rg + 1)],
                                PT[b2][0:CH, 512 * g + 256 * ch:512 * g + 256 * (ch + 1)]
                                .rearrange("p (e t) -> p e t", e=H2)[:, :, T * rg:T * (rg + 1)],
                                start=(ch == 0), stop=(ch == 1), tile_position=(0, HD * g), skip_group_check=True)
                ins.then_inc(summed_o, 1)

            def spread_r(n, b2):
                pe.wait_ge(r_set, n + 1)
                if not isinstance(n, int) or n >= 1:
                    pe.wait_ge(y_set, n)
                for e in range(H2):
                    ins = pe.transpose(R_PS[:, P * e:P * (e + 1)], R32[b2][:, P * e:P * (e + 1)], ident)
                ins.then_inc(r_spread, 1)

            def project_o(n, b2):
                pe.wait_ge(o_scaled, n + 1)
                for e in range(H2):
                    ins = pe.matmul(Y_PS, AT[b2][:, P * e:P * (e + 1)], WO_T[:, D * e:D * (e + 1)],
                                    start=(e == 0), stop=(e == H2 - 1))
                ins.then_inc(y_done, 1)

            def stage(n, m):
                b2, p, p_prev = m % 2, m // 2 % 2, (m - 1) // 2 % 2
                loop = not isinstance(n, int)
                new, prev, old = loop or n < NT, loop or 1 <= n <= NT, loop or 2 <= n < NT + 2
                if new:
                    if b2 == 0:
                        pe.wait_ge(kt_set, n + 1)
                    pe.wait_ge(qd_set, n + 1)
                    score(n, b2, p, 0)
                for g in range(G):
                    if old and g == 1:
                        attend(n - 2, b2)
                        spread_r(n - 2, b2)
                    if prev and g in (1, 3):
                        if b2 == 1 and g == 1:
                            pe.wait_ge(vt_set, n + 1)
                        turn_v(n - 1, 1 - b2, p_prev, int(g == 3))
                    if prev:
                        turn_p(n - 1, 1 - b2, g)
                    if new and g + 1 < G:
                        if b2 == 0 and g == 1:
                            pe.wait_ge(kt_set, n + 2)
                        score(n, b2, p, g + 1)
                if old:
                    project_o(n - 2, b2)

            for n in range(4):
                stage(n, n)
            with pe.Fori(1, NT // 4) as i:
                for m in range(4):
                    stage(4 * i + m, m)
            for n in range(NT, NT + 2):
                stage(n, n % 4)


def kernel(x, itok_B_1_198, itok_Bx257_0_4111, itok_B_37_3939, L0_cond_weights, L1_cond_Wq, L1_cond_Wk, L1_cond_Wv,
           L1_cond_Wo, L1_cond_q_norm_scale, L1_cond_k_norm_scale, L1_cond_k_blocks, L1_cond_v_blocks):
    import concourse.bacc as bacc
    from concourse.bass_utils import run_bass_kernel_spmd

    nc = bacc.Bacc("TRN2", target_bir_lowering=False, num_devices=1)
    table, at = constants()
    ins = {
        "x": x, "cond": itok_B_1_198, "table": itok_Bx257_0_4111, "kv_lens": itok_B_37_3939, "l0_w": L0_cond_weights,
        "wq": L1_cond_Wq, "wk": L1_cond_Wk, "wv": L1_cond_Wv, "wo": L1_cond_Wo,
        "q_scale": L1_cond_q_norm_scale, "k_scale": L1_cond_k_norm_scale,
        "k_blocks": L1_cond_k_blocks, "v_blocks": L1_cond_v_blocks, "consts": table,
    }
    arrays = {f"in_{n}": np.ascontiguousarray(a) for n, a in ins.items()}
    aps = {n: nc.dram_tensor(f"in_{n}", a.shape, mybir.dt.from_np(a.dtype), kind="ExternalInput").ap()
           for n, a in ((k[3:], v) for k, v in arrays.items())}
    out = nc.dram_tensor("out", (B, T, D), F32, kind="ExternalOutput").ap()
    build(nc, at, out=out, **aps)
    return run_bass_kernel_spmd(nc, [arrays], core_ids=[0]).results[0]["out"]
```
